# Optimizing a Trainium2 kernel written in Bass

```python
import numpy as np
import jax
import jax.numpy as jnp

def _softmax(x, axis=-1):
    return jax.nn.softmax(x, axis=axis)

def _gelu(x):
    return jax.nn.gelu(x, approximate=True)

def _silu(x):
    return jax.nn.silu(x)

def _sigmoid(x):
    return jax.nn.sigmoid(x)

def _layernorm(x, axis=-1, eps=1e-05):
    m = jnp.mean(x, axis=axis, keepdims=True)
    v = jnp.var(x, axis=axis, keepdims=True)
    return (x - m) / jnp.sqrt(v + eps)

def _scatter_add(tgt, idx, src, axis=0):
    return tgt.at[idx].add(src)

def _segment_sum(src, seg, n):
    return jax.ops.segment_sum(src, seg, n)
kernel_name = 'mk_dlrm_tower_d1_rec_r8_6a2ced'

def setup_inputs(seed: int=0):
    np.random.seed(seed)
    _w = jnp.asarray

    def _rec_inputs():
        import jax
        import jax.numpy as jnp
        _tk = jax.random.key(seed)
        dense_ctx = jax.random.normal(jax.random.fold_in(_tk, 190), (2048, 16), jnp.float32)
        ids = jnp.stack([jax.random.randint(jax.random.fold_in(_tk, 200 + f), (2048,), 0, v, jnp.int32) for f, v in enumerate([125000, 125000, 1250, 12500, 125000, 12500, 12500, 125000, 1250, 125000, 125000, 1000, 12500, 12500, 1000, 1250, 125000, 125000, 12500, 1000, 1000, 12500, 12500, 125000, 1000, 12500, 1250, 1250, 1250, 125000, 1000, 1000, 125000, 125000, 12500, 125000, 12500, 12500, 1250])], axis=1)
        tbl_0 = 0.05 * jax.random.normal(jax.random.fold_in(_tk, 500 + 0), (125000, 16), jnp.float32)
        tbl_1 = 0.05 * jax.random.normal(jax.random.fold_in(_tk, 500 + 1), (125000, 16), jnp.float32)
        tbl_2 = 0.05 * jax.random.normal(jax.random.fold_in(_tk, 500 + 2), (1250, 16), jnp.float32)
        tbl_3 = 0.05 * jax.random.normal(jax.random.fold_in(_tk, 500 + 3), (12500, 16), jnp.float32)
        tbl_4 = 0.05 * jax.random.normal(jax.random.fold_in(_tk, 500 + 4), (125000, 16), jnp.float32)
        tbl_5 = 0.05 * jax.random.normal(jax.random.fold_in(_tk, 500 + 5), (12500, 16), jnp.float32)
        tbl_6 = 0.05 * jax.random.normal(jax.random.fold_in(_tk, 500 + 6), (12500, 16), jnp.float32)
        tbl_7 = 0.05 * jax.random.normal(jax.random.fold_in(_tk, 500 + 7), (125000, 16), jnp.float32)
        tbl_8 = 0.05 * jax.random.normal(jax.random.fold_in(_tk, 500 + 8), (1250, 16), jnp.float32)
        tbl_9 = 0.05 * jax.random.normal(jax.random.fold_in(_tk, 500 + 9), (125000, 16), jnp.float32)
        tbl_10 = 0.05 * jax.random.normal(jax.random.fold_in(_tk, 500 + 10), (125000, 16), jnp.float32)
        tbl_11 = 0.05 * jax.random.normal(jax.random.fold_in(_tk, 500 + 11), (1000, 16), jnp.float32)
        tbl_12 = 0.05 * jax.random.normal(jax.random.fold_in(_tk, 500 + 12), (12500, 16), jnp.float32)
        tbl_13 = 0.05 * jax.random.normal(jax.random.fold_in(_tk, 500 + 13), (12500, 16), jnp.float32)
        tbl_14 = 0.05 * jax.random.normal(jax.random.fold_in(_tk, 500 + 14), (1000, 16), jnp.float32)
        tbl_15 = 0.05 * jax.random.normal(jax.random.fold_in(_tk, 500 + 15), (1250, 16), jnp.float32)
        tbl_16 = 0.05 * jax.random.normal(jax.random.fold_in(_tk, 500 + 16), (125000, 16), jnp.float32)
        tbl_17 = 0.05 * jax.random.normal(jax.random.fold_in(_tk, 500 + 17), (125000, 16), jnp.float32)
        tbl_18 = 0.05 * jax.random.normal(jax.random.fold_in(_tk, 500 + 18), (12500, 16), jnp.float32)
        tbl_19 = 0.05 * jax.random.normal(jax.random.fold_in(_tk, 500 + 19), (1000, 16), jnp.float32)
        tbl_20 = 0.05 * jax.random.normal(jax.random.fold_in(_tk, 500 + 20), (1000, 16), jnp.float32)
        tbl_21 = 0.05 * jax.random.normal(jax.random.fold_in(_tk, 500 + 21), (12500, 16), jnp.float32)
        tbl_22 = 0.05 * jax.random.normal(jax.random.fold_in(_tk, 500 + 22), (12500, 16), jnp.float32)
        tbl_23 = 0.05 * jax.random.normal(jax.random.fold_in(_tk, 500 + 23), (125000, 16), jnp.float32)
        tbl_24 = 0.05 * jax.random.normal(jax.random.fold_in(_tk, 500 + 24), (1000, 16), jnp.float32)
        tbl_25 = 0.05 * jax.random.normal(jax.random.fold_in(_tk, 500 + 25), (12500, 16), jnp.float32)
        tbl_26 = 0.05 * jax.random.normal(jax.random.fold_in(_tk, 500 + 26), (1250, 16), jnp.float32)
        tbl_27 = 0.05 * jax.random.normal(jax.random.fold_in(_tk, 500 + 27), (1250, 16), jnp.float32)
        tbl_28 = 0.05 * jax.random.normal(jax.random.fold_in(_tk, 500 + 28), (1250, 16), jnp.float32)
        tbl_29 = 0.05 * jax.random.normal(jax.random.fold_in(_tk, 500 + 29), (125000, 16), jnp.float32)
        tbl_30 = 0.05 * jax.random.normal(jax.random.fold_in(_tk, 500 + 30), (1000, 16), jnp.float32)
        tbl_31 = 0.05 * jax.random.normal(jax.random.fold_in(_tk, 500 + 31), (1000, 16), jnp.float32)
        tbl_32 = 0.05 * jax.random.normal(jax.random.fold_in(_tk, 500 + 32), (125000, 16), jnp.float32)
        tbl_33 = 0.05 * jax.random.normal(jax.random.fold_in(_tk, 500 + 33), (125000, 16), jnp.float32)
        tbl_34 = 0.05 * jax.random.normal(jax.random.fold_in(_tk, 500 + 34), (12500, 16), jnp.float32)
        tbl_35 = 0.05 * jax.random.normal(jax.random.fold_in(_tk, 500 + 35), (125000, 16), jnp.float32)
        tbl_36 = 0.05 * jax.random.normal(jax.random.fold_in(_tk, 500 + 36), (12500, 16), jnp.float32)
        tbl_37 = 0.05 * jax.random.normal(jax.random.fold_in(_tk, 500 + 37), (12500, 16), jnp.float32)
        tbl_38 = 0.05 * jax.random.normal(jax.random.fold_in(_tk, 500 + 38), (1250, 16), jnp.float32)
        _rk = jax.random.fold_in(_tk, 7)
        W_top1 = 0.0606339 * jax.random.normal(jax.random.fold_in(_tk, 801), (272, 512), jnp.float32)
        W_top2 = 0.0441942 * jax.random.normal(jax.random.fold_in(_tk, 802), (512, 256), jnp.float32)
        W_top3 = 0.0625 * jax.random.normal(jax.random.fold_in(_tk, 803), (256, 1), jnp.float32)
        b_top1 = jnp.zeros((512,), jnp.float32)
        b_top2 = jnp.zeros((256,), jnp.float32)
        return (dense_ctx, ids, tbl_0, tbl_1, tbl_2, tbl_3, tbl_4, tbl_5, tbl_6, tbl_7, tbl_8, tbl_9, tbl_10, tbl_11, tbl_12, tbl_13, tbl_14, tbl_15, tbl_16, tbl_17, tbl_18, tbl_19, tbl_20, tbl_21, tbl_22, tbl_23, tbl_24, tbl_25, tbl_26, tbl_27, tbl_28, tbl_29, tbl_30, tbl_31, tbl_32, tbl_33, tbl_34, tbl_35, tbl_36, tbl_37, tbl_38, W_top1, b_top1, W_top2, b_top2, W_top3)
    dense_ctx, ids, tbl_0, tbl_1, tbl_2, tbl_3, tbl_4, tbl_5, tbl_6, tbl_7, tbl_8, tbl_9, tbl_10, tbl_11, tbl_12, tbl_13, tbl_14, tbl_15, tbl_16, tbl_17, tbl_18, tbl_19, tbl_20, tbl_21, tbl_22, tbl_23, tbl_24, tbl_25, tbl_26, tbl_27, tbl_28, tbl_29, tbl_30, tbl_31, tbl_32, tbl_33, tbl_34, tbl_35, tbl_36, tbl_37, tbl_38, W_top1, b_top1, W_top2, b_top2, W_top3 = _rec_inputs()

    def _L0_rec_setup():
        import jax, jax.numpy as jnp
        import numpy as np
        B, F0, D = (256, 39, 16)
        LAYER_SIZES = [128, 128, 128]
        key = jax.random.key(seed)
        ks = jax.random.split(key, 1 + 2 * len(LAYER_SIZES))
        inputs = jax.random.normal(ks[0], (B, F0, D), dtype=jnp.float32)
        out = {'inputs': inputs}
        field_nums = [F0]
        for i, size in enumerate(LAYER_SIZES):
            fk = field_nums[-1]
            fan_in = F0 * fk
            scale = np.sqrt(2.0 / (fan_in + size)).astype(np.float32)
            out[f'w{i}'] = jax.random.normal(ks[1 + 2 * i], (F0, fk, size), dtype=jnp.float32) * scale
            out[f'b{i}'] = jnp.zeros((size,), dtype=jnp.float32)
            field_nums.append(size // 2)
        return out
    _L0_rec_all = _L0_rec_setup()
    _L0_rec_in = {k: v for k, v in _L0_rec_all.items() if k in ('w0', 'w1', 'w2', 'b0', 'b1', 'b2')}
    del _L0_rec_all
    return {'dense_ctx': dense_ctx, 'ids': ids, 'tbl_0': tbl_0, 'tbl_1': tbl_1, 'tbl_2': tbl_2, 'tbl_3': tbl_3, 'tbl_4': tbl_4, 'tbl_5': tbl_5, 'tbl_6': tbl_6, 'tbl_7': tbl_7, 'tbl_8': tbl_8, 'tbl_9': tbl_9, 'tbl_10': tbl_10, 'tbl_11': tbl_11, 'tbl_12': tbl_12, 'tbl_13': tbl_13, 'tbl_14': tbl_14, 'tbl_15': tbl_15, 'tbl_16': tbl_16, 'tbl_17': tbl_17, 'tbl_18': tbl_18, 'tbl_19': tbl_19, 'tbl_20': tbl_20, 'tbl_21': tbl_21, 'tbl_22': tbl_22, 'tbl_23': tbl_23, 'tbl_24': tbl_24, 'tbl_25': tbl_25, 'tbl_26': tbl_26, 'tbl_27': tbl_27, 'tbl_28': tbl_28, 'tbl_29': tbl_29, 'tbl_30': tbl_30, 'tbl_31': tbl_31, 'tbl_32': tbl_32, 'tbl_33': tbl_33, 'tbl_34': tbl_34, 'tbl_35': tbl_35, 'tbl_36': tbl_36, 'tbl_37': tbl_37, 'tbl_38': tbl_38, 'W_top1': W_top1, 'b_top1': b_top1, 'W_top2': W_top2, 'b_top2': b_top2, 'W_top3': W_top3, 'L0_rec_w0': _L0_rec_in['w0'], 'L0_rec_w1': _L0_rec_in['w1'], 'L0_rec_w2': _L0_rec_in['w2'], 'L0_rec_b0': _L0_rec_in['b0'], 'L0_rec_b1': _L0_rec_in['b1'], 'L0_rec_b2': _L0_rec_in['b2']}

def reference(dense_ctx, ids, tbl_0, tbl_1, tbl_2, tbl_3, tbl_4, tbl_5, tbl_6, tbl_7, tbl_8, tbl_9, tbl_10, tbl_11, tbl_12, tbl_13, tbl_14, tbl_15, tbl_16, tbl_17, tbl_18, tbl_19, tbl_20, tbl_21, tbl_22, tbl_23, tbl_24, tbl_25, tbl_26, tbl_27, tbl_28, tbl_29, tbl_30, tbl_31, tbl_32, tbl_33, tbl_34, tbl_35, tbl_36, tbl_37, tbl_38, W_top1, b_top1, W_top2, b_top2, W_top3, L0_rec_w0, L0_rec_w1, L0_rec_w2, L0_rec_b0, L0_rec_b1, L0_rec_b2):
    import jax
    import jax.numpy as jnp

    def _L0_rec_ref(inputs, w0, w1, w2, b0, b1, b2):
        import jax, jax.numpy as jnp
        import numpy as np
        B, F0, D = (256, 39, 16)
        LAYER_SIZES = [128, 128, 128]
        x0 = inputs
        xk = inputs
        params = [(w0, b0), (w1, b1), (w2, b2)]
        n_layers = len(params)
        direct = []
        for idx, (W, b) in enumerate(params):
            z = jnp.einsum('bhd,bkd,hks->bsd', x0, xk, W) + b[None, :, None]
            z = jax.nn.relu(z)
            if idx != n_layers - 1:
                half = z.shape[1] // 2
                xk = z[:, :half, :]
                direct.append(z[:, half:, :])
            else:
                direct.append(z)
        logit = jnp.sum(jnp.concatenate(direct, axis=1), axis=-1)
        return logit
    e = jnp.stack([tbl_0[ids[:, 0]], tbl_1[ids[:, 1]], tbl_2[ids[:, 2]], tbl_3[ids[:, 3]], tbl_4[ids[:, 4]], tbl_5[ids[:, 5]], tbl_6[ids[:, 6]], tbl_7[ids[:, 7]], tbl_8[ids[:, 8]], tbl_9[ids[:, 9]], tbl_10[ids[:, 10]], tbl_11[ids[:, 11]], tbl_12[ids[:, 12]], tbl_13[ids[:, 13]], tbl_14[ids[:, 14]], tbl_15[ids[:, 15]], tbl_16[ids[:, 16]], tbl_17[ids[:, 17]], tbl_18[ids[:, 18]], tbl_19[ids[:, 19]], tbl_20[ids[:, 20]], tbl_21[ids[:, 21]], tbl_22[ids[:, 22]], tbl_23[ids[:, 23]], tbl_24[ids[:, 24]], tbl_25[ids[:, 25]], tbl_26[ids[:, 26]], tbl_27[ids[:, 27]], tbl_28[ids[:, 28]], tbl_29[ids[:, 29]], tbl_30[ids[:, 30]], tbl_31[ids[:, 31]], tbl_32[ids[:, 32]], tbl_33[ids[:, 33]], tbl_34[ids[:, 34]], tbl_35[ids[:, 35]], tbl_36[ids[:, 36]], tbl_37[ids[:, 37]], tbl_38[ids[:, 38]]], axis=1)
    z = _L0_rec_ref(e, L0_rec_w0, L0_rec_w1, L0_rec_w2, L0_rec_b0, L0_rec_b1, L0_rec_b2)
    z = z.reshape(z.shape[0], -1)
    h = jnp.concatenate([z, dense_ctx], axis=1)
    h = jnp.maximum(h @ W_top1 + b_top1, 0.0)
    h = jnp.maximum(h @ W_top2 + b_top2, 0.0)
    y = h @ W_top3
    return y

_drawn_inputs = setup_inputs


def setup_inputs(seed=0):
    import zlib

    import numpy as np

    out = dict(_drawn_inputs(seed))
    spreads = {'b_top1': (0.0, 2.0),
     'b_top2': (0.0, 2.0),
     'L0_rec_b0': (0.0, 0.35),
     'L0_rec_b1': (0.0, 0.532),
     'L0_rec_b2': (0.0, 0.8)}
    factors = {'tbl_0': 8.0,
     'tbl_1': 8.0,
     'tbl_2': 8.0,
     'tbl_3': 8.0,
     'tbl_4': 8.0,
     'tbl_5': 8.0,
     'tbl_6': 8.0,
     'tbl_7': 8.0,
     'tbl_8': 8.0,
     'tbl_9': 8.0,
     'tbl_10': 8.0,
     'tbl_11': 8.0,
     'tbl_12': 8.0,
     'tbl_13': 8.0,
     'tbl_14': 8.0,
     'tbl_15': 8.0,
     'tbl_16': 8.0,
     'tbl_17': 8.0,
     'tbl_18': 8.0,
     'tbl_19': 8.0,
     'tbl_20': 8.0,
     'tbl_21': 8.0,
     'tbl_22': 8.0,
     'tbl_23': 8.0,
     'tbl_24': 8.0,
     'tbl_25': 8.0,
     'tbl_26': 8.0,
     'tbl_27': 8.0,
     'tbl_28': 8.0,
     'tbl_29': 8.0,
     'tbl_30': 8.0,
     'tbl_31': 8.0,
     'tbl_32': 8.0,
     'tbl_33': 8.0,
     'tbl_34': 8.0,
     'tbl_35': 8.0,
     'tbl_36': 8.0,
     'tbl_37': 8.0,
     'tbl_38': 8.0,
     'L0_rec_w0': 8.0,
     'L0_rec_w1': 6.216,
     'L0_rec_w2': 4.698,
     'dense_ctx': 8.0}
    for name, (base, spread) in spreads.items():
        noise = np.random.default_rng([zlib.crc32(name.encode()), seed]).standard_normal(out[name].shape)
        drawn = base * np.exp(spread * noise) if base else spread * noise
        out[name] = jnp.asarray(drawn.astype(out[name].dtype))
    for name, factor in factors.items():
        out[name] = (out[name] * factor).astype(out[name].dtype)
    return out
```

```python
from contextlib import ExitStack

import numpy as np

import concourse.bass as bass
from concourse import mybir

FIELDS, DIM, BATCH = 39, 16, 2048
SIZE = 128
KEPT = SIZE // 2
ROWS = 128
BLOCKS = BATCH // ROWS
HALF = DIM // 2 * ROWS
BLOCK_COLS = DIM * ROWS
BANK = 512
SHIFTS = FIELDS // 2 + 1
PER_UNIT = 3
PAIR_ROWS = FIELDS * PER_UNIT
UNITS_0 = -(-SHIFTS // PER_UNIT)
UNITS_K = -(-FIELDS * KEPT // 128)
CONTEXT, TOP1, TOP2 = 16, 512, 256

UNITS = {0: UNITS_0, 1: UNITS_K, 2: UNITS_K}
SPLIT = {0: (1, 3, 5), 1: (1, 4, 7, 10, 12, 14, 17), 2: (1, 4, 7, 10, 12, 14, 17)}
P_RING, PART_RING, PAIR_RING = 4, 2, 3
LAG = 1
EVAC_AT = 3


def contraction(layer, t):
    return PAIR_ROWS if layer == 0 else min(128, FIELDS * KEPT - 128 * t)


class Unit:
    def __init__(self, layer, t, phase, n, s):
        self.layer, self.t, self.phase, self.n = layer, t, phase, n
        self.rows = contraction(layer, t)
        self.split = t in SPLIT[layer]
        self.s = s


class Section:

    def __init__(self, phases, last=False, first=False):
        self.phases, self.units, self.first = phases, [], first
        s = 0
        for ph, (layer, half) in enumerate(phases):
            for t in range(UNITS[layer]):
                self.units.append(Unit(layer, t, ph, len(self.units), s))
                s += self.units[-1].split
        self.splits = s
        self.n_shift = 0 if last else len(self.units)
        self.s_shift = 0 if last else s
        self.tail = [Unit(1, t, -1, t - UNITS_K, sum(x < t for x in SPLIT[1]) - len(SPLIT[1]))
                     for t in range(UNITS_K)]

    def at(self, phase, t):
        return next(u.n for u in self.units if u.phase == phase and u.t == t)

    def needs_last_phase(self, phase):
        if phase == 0:
            return False
        layer, half = self.phases[phase]
        return self.phases[phase - 1] == (layer - 1, half)

    def p_slot(self, u):
        return u.n % P_RING if u.n < 0 else (u.n - self.n_shift) % P_RING

    def part_slot(self, u):
        return u.s % PART_RING if u.n < 0 else (u.s - self.s_shift) % PART_RING

    def before(self, u, slot, chosen):
        known = ([] if self.first else self.tail) + self.units
        same = [x for x in known if x.n < u.n and chosen(x) and slot(x) == slot(u)]
        return same[-1] if same else None


A, B = 0, 1
FIRST = Section([(0, A), (1, A)], first=True)
LOOP = Section([(0, B), (2, A), (1, B), (0, A), (2, B), (1, A)])
LAST = Section([(0, B), (2, A), (1, B), (2, B)], last=True)


def counts_before(section, j):
    if section is FIRST:
        return 0, 0, 0
    return (j * len(LOOP.units) + len(FIRST.units), j * LOOP.splits + FIRST.splits,
            j * len(LOOP.phases) + len(FIRST.phases))


def halves_before(section, phase, j):
    if section is FIRST:
        return 0
    return j * 2 + (1 if section.phases[phase][1] == B else 2)


def build(nc, ids, tables, w0, w0_mirror, w1, w2, bias0, bias1, bias2,
          top1, top1_context, top2, top3, top_bias1, top_bias2, context, eye, out):
    f32, f32r, i32, u32 = mybir.dt.float32, mybir.dt.float32r, mybir.dt.int32, mybir.dt.uint32
    ALU, ACT, AX = mybir.AluOpType, mybir.ActivationFunctionType, mybir.AxisListType

    whole_list = [(l, t) for l in UNITS for t in range(UNITS[l]) if t not in SPLIT[l]]
    split_list = [(l, t) for l in UNITS for t in range(UNITS[l]) if t in SPLIT[l]]
    out_rows = out.rearrange("(a b) c -> a (b c)", b=ROWS)

    x0_dram = nc.dram_tensor("x0_dram", [BLOCKS, 2 * FIELDS, BLOCK_COLS], f32)

    with ExitStack() as ctx:
        def sb(name, shape, dtype=f32):
            return ctx.enter_context(nc.sbuf_tensor(name, shape, dtype))

        def sem(name):
            return ctx.enter_context(nc.semaphore(name))

        x0_rep = sb("x0_rep", [128, UNITS_K, HALF])
        pair_rep = sb("pair_rep", [PAIR_ROWS, HALF])
        pair_shift = sb("pair_shift", [PAIR_ROWS, PAIR_RING, HALF])
        x1 = sb("x1", [128, HALF])
        x2 = sb("x2", [128, HALF])
        direct01 = sb("direct01", [128, HALF])
        direct2 = sb("direct2", [128, HALF])
        prod = sb("prod", [128, P_RING, HALF])
        prod_hi = sb("prod_hi", [128, PART_RING, HALF], f32r)
        prod_lo = sb("prod_lo", [128, PART_RING, HALF], f32r)
        w_whole = sb("w_whole", [128, len(whole_list), SIZE])
        w_hi = sb("w_hi", [128, len(split_list), SIZE], f32r)
        w_lo = sb("w_lo", [128, len(split_list), SIZE], f32r)
        ids_sb = sb("ids_sb", [ROWS, FIELDS], i32)
        emb = sb("emb", [ROWS, FIELDS * DIM])
        x0_sb = sb("x0_sb", [2 * FIELDS, HALF])
        sums = sb("sums", [128, 2, ROWS])
        part_sums = sb("part_sums", [128, 2, ROWS])
        context_sb = sb("context_sb", [CONTEXT, ROWS])
        top1_sb = sb("top1_sb", [128, 2, TOP1])
        top1c_sb = sb("top1c_sb", [CONTEXT, TOP1])
        top2_sb = sb("top2_sb", [128, TOP1 // 128, TOP2])
        top3_sb = sb("top3_sb", [128, TOP2 // 128])
        tb1_sb = sb("tb1_sb", [128, TOP1 // 128])
        tb2_sb = sb("tb2_sb", [128, TOP2 // 128])
        bias_sb = sb("bias_sb", [128, 3])
        h1 = sb("h1", [128, TOP1 // 128, ROWS])
        h2 = sb("h2", [128, TOP2 // 128, ROWS])
        y_sb = sb("y_sb", [1, ROWS])
        eye_sb = sb("eye_sb", [128, 128])

        acc = ctx.enter_context(nc.psum_tensor("acc", [128, 2, HALF], f32))
        turned = ctx.enter_context(nc.psum_tensor("turned", [128, 2, BANK], f32))
        top_a = ctx.enter_context(nc.psum_tensor("top_a", [128, TOP1 // 128, ROWS], f32))
        top_b = ctx.enter_context(nc.psum_tensor("top_b", [128, TOP1 // 128, ROWS], f32))

        raw = x0_rep[:, :, 0:SIZE]
        raw_direct = x0_rep[:, :, SIZE:2 * SIZE]
        raw_mirror = x0_rep[:, :, 2 * SIZE:3 * SIZE]

        consts_loaded = sem("consts_loaded")
        cin_weights_loaded = sem("cin_weights_loaded")
        pair_sums_ready = sem("pair_sums_ready")
        w_hi_ready = sem("w_hi_ready")
        weights_ready = sem("weights_ready")
        ids_loaded = sem("ids_loaded")
        gathered = sem("gathered")
        turned_ready = sem("turned_ready")
        turned_taken = sem("turned_taken")
        x0_stored = sem("x0_stored")
        pair_rep_loaded = sem("pair_rep_loaded")
        shift_loaded = [sem(f"shift_loaded{r}") for r in range(PAIR_RING)]
        x0_rep_loaded = [sem(f"x0_rep_loaded{t}") for t in range(UNITS_K)]
        prod_ready = sem("prod_ready")
        hi_ready = sem("hi_ready")
        lo_ready = sem("lo_ready")
        unit_done = sem("unit_done")
        phase_taken = sem("phase_taken")
        half_reduced = sem("half_reduced")
        sums_ready = sem("sums_ready")
        context_loaded = sem("context_loaded")
        top1_done, top2_done, top3_done = sem("top1_done"), sem("top2_done"), sem("top3_done")
        h1_ready, h2_ready, y_ready = sem("h1_ready"), sem("h2_ready"), sem("y_ready")
        y_stored = sem("y_stored")
        waited, gather_waited = sem("waited"), sem("gather_waited")

        N_CONSTS = 10
        N_CIN = 2 * UNITS_0 + 2 * UNITS_K
        TURNS = HALF // BANK

        block = ctx.enter_context(nc.Block())

        @block.sync
        def _(sp):
            for l in (0, 1, 2):
                for t in range(UNITS[l]):
                    rows = contraction(l, t)
                    if l == 0:
                        sp.dma_start(raw_direct[0:rows, t, :], w0[t]).then_inc(cin_weights_loaded, 16)
                        sp.dma_start(raw_mirror[0:rows, t, :], w0_mirror[t]).then_inc(cin_weights_loaded, 16)
                        continue
                    if (l, t) in whole_list:
                        to = w_whole[0:rows, whole_list.index((l, t)), :]
                    else:
                        to = raw[0:rows, split_list.index((l, t)), :]
                    src = (w1, w2)[l - 1]
                    sp.dma_start(to, src[128 * t:128 * t + rows, :]).then_inc(cin_weights_loaded, 16)

            def load_pair_rep(j, half, before):
                base = x0_dram[bass.ds(j, 1), 0:1, half * HALF:(half + 1) * HALF]
                src = bass.AP(base.tensor, base.offset, [[BLOCK_COLS, FIELDS], [0, PER_UNIT], [1, HALF]])
                if before is not None:
                    sp.wait_ge(prod_ready, before)
                    sp.sem_inc(waited, 1)
                sp.dma_start(pair_rep[:], src).then_inc(pair_rep_loaded, 16)

            def load_shift(j, half, t, before):
                base = x0_dram[bass.ds(j, 1), PER_UNIT * t:PER_UNIT * t + 1, half * HALF:(half + 1) * HALF]
                src = bass.AP(base.tensor, base.offset,
                              [[BLOCK_COLS, FIELDS], [BLOCK_COLS, PER_UNIT], [1, HALF]])
                if before is not None:
                    sp.wait_ge(prod_ready, before)
                    sp.sem_inc(waited, 1)
                sp.dma_start(pair_shift[:, t % PAIR_RING, :], src).then_inc(shift_loaded[t % PAIR_RING], 16)

            def load_x0_rep(j, half, t, before):
                if before is not None:
                    sp.wait_ge(prod_ready, before)
                    sp.sem_inc(waited, 1)
                for r in range(contraction(1, t) // KEPT):
                    h = 2 * t + r
                    row = x0_dram[bass.ds(j, 1), h:h + 1, half * HALF:(half + 1) * HALF]
                    sp.dma_start(x0_rep[r * KEPT:(r + 1) * KEPT, t, :],
                                 row.rearrange("a p n -> (a p) n").to_broadcast([KEPT, HALF])
                                 ).then_inc(x0_rep_loaded[t], 16)

            def store_x0(j):
                sp.wait_ge(turned_taken, TURNS * (j + 1))
                sp.sem_inc(waited, 1)
                for copy in (0, 1):
                    to = x0_dram[bass.ds(j, 1), copy * FIELDS:(copy + 1) * FIELDS, :]
                    sp.dma_start(to.rearrange("a f (h n) -> (a f h) n", h=2), x0_sb[:]).then_inc(x0_stored, 16)
                sp.wait_ge(x0_stored, 32 * (j + 1))
                sp.sem_inc(waited, 1)

            def load_layer0(j, half, section, phase, section_j):
                units = counts_before(section, section_j)[0]
                at = section.at(phase, 0)
                before = None if section is FIRST else units + at - UNITS_K
                load_pair_rep(j, half, before)
                for t in range(UNITS_0):
                    load_shift(j, half, t, None if t < PAIR_RING else units + at + t - PAIR_RING + 1)

            for dst, src in ((eye_sb[:], eye), (bias_sb[:, 0:1], bias0), (bias_sb[:, 1:2], bias1),
                             (bias_sb[:, 2:3], bias2)):
                sp.dma_start(dst, src).then_inc(consts_loaded, 16)
            for dst, src in ((top1_sb[:], top1), (top1c_sb[:], top1_context), (top2_sb[:], top2),
                             (top3_sb[:], top3), (tb1_sb[:], top_bias1), (tb2_sb[:], top_bias2)):
                sp.dma_start(dst, src).then_inc(consts_loaded, 16)
            sp.dma_start(context_sb[:], context[0]).then_inc(context_loaded, 16)

            store_x0(0)
            load_layer0(0, A, FIRST, 0, None)
            sp.wait_ge(weights_ready, 1)
            for t in range(UNITS_K):
                load_x0_rep(0, A, t, None)

            def section_loads(j, section):
                units = counts_before(section, j)[0]
                load_layer0(j, B, section, 0, j)
                if section is LOOP:
                    store_x0(j + 1)
                for t in range(UNITS_K):
                    load_x0_rep(j, B, t, units + section.at(1, t) + 1)
                if section is LOOP:
                    load_layer0(j + 1, A, section, 3, j)
                    for t in range(UNITS_K):
                        load_x0_rep(j + 1, A, t, units + section.at(4, t) + 1)
                    sp.wait_ge(top1_done, j + 1)
                    sp.sem_inc(waited, 1)
                    sp.dma_start(context_sb[:], context[bass.ds(j + 1, 1)].rearrange("a p n -> (a p) n")
                                 ).then_inc(context_loaded, 16)

            with sp.Fori(0, BLOCKS - 1) as j:
                section_loads(j, LOOP)
            section_loads(BLOCKS - 1, LAST)

        @block.gpsimd
        def _(pool):
            def gather(j):
                pool.dma_start(ids_sb[:], ids[bass.ds(j * ROWS, ROWS), :]).then_inc(ids_loaded, 16)
                pool.wait_ge(ids_loaded, 16 * (j + 1))
                pool.sem_inc(gather_waited, 1)
                for f in range(FIELDS):
                    pool.indirect_dma_start(
                        out=emb[:, f * DIM:(f + 1) * DIM], out_offset=None, in_=tables[f],
                        in_offset=bass.IndirectOffsetOnAxis(ap=ids_sb[:, f:f + 1].bitcast(u32), axis=0),
                    ).then_inc(gathered, 16)

            gather(0)
            with pool.Fori(1, BLOCKS) as j:
                pool.wait_ge(gathered, 16 * FIELDS * j)
                pool.wait_ge(turned_ready, TURNS * j)
                gather(j)

        @block.vector
        def _(dve):
            dve.wait_ge(cin_weights_loaded, 16 * N_CIN)
            for t in range(UNITS_0):
                if (0, t) in whole_list:
                    to = w_whole[0:PAIR_ROWS, whole_list.index((0, t)), :]
                else:
                    to = raw[0:PAIR_ROWS, split_list.index((0, t)), :]
                nc.vector.tensor_tensor(to, raw_direct[0:PAIR_ROWS, t, :], raw_mirror[0:PAIR_ROWS, t, :],
                                        ALU.add).then_inc(pair_sums_ready, 1)
            dve.wait_ge(pair_sums_ready, UNITS_0)
            for k, (l, t) in enumerate(split_list):
                rows = contraction(l, t)
                nc.vector.tensor_copy(w_hi[0:rows, k, :], raw[0:rows, k, :]).then_inc(w_hi_ready, 1)
            dve.wait_ge(w_hi_ready, len(split_list))
            for k, (l, t) in enumerate(split_list):
                rows = contraction(l, t)
                last = nc.vector.tensor_tensor(w_lo[0:rows, k, :], raw[0:rows, k, :],
                                               w_hi[0:rows, k, :].bitcast(f32), ALU.subtract)
            last.then_inc(weights_ready, 1)

            def low_part(section, u, units, splits):
                if (old := section.before(u, section.part_slot, lambda x: x.split)) is not None:
                    dve.wait_ge(unit_done, units + old.n + 1)
                dve.wait_ge(prod_ready, units + u.n + 1)
                dve.wait_ge(hi_ready, splits + u.s + 1)
                nc.vector.tensor_tensor(prod_lo[0:u.rows, section.part_slot(u), :],
                                        prod[0:u.rows, section.p_slot(u), :],
                                        prod_hi[0:u.rows, section.part_slot(u), :].bitcast(f32),
                                        ALU.subtract).then_inc(lo_ready, 1)

            def reduce_half(j, n, which, half, phase_no):
                src = (direct01, direct2)[which]
                dst = (sums, part_sums)[half]
                dve.wait_ge(phase_taken, phase_no)
                nc.vector.tensor_reduce(dst[:, which, :], src[:].rearrange("p (d b) -> p b d", b=ROWS),
                                        AX.X, ALU.add).then_inc(half_reduced, 1)
                if half == B:
                    dve.wait_ge(half_reduced, j * 4 + n)
                    nc.vector.tensor_tensor(sums[:, which, :], sums[:, which, :],
                                            part_sums[:, which, :], ALU.add).then_inc(sums_ready, 1)

            def section_products(j, section, events):
                units, splits, phases = counts_before(section, j)
                waiting = []
                for u in section.units:
                    if u.t == 0 and u.layer > 0:
                        half = section.phases[u.phase][1]
                        source = next((p for p in reversed(range(u.phase))
                                       if section.phases[p] == (u.layer - 1, half)), -1)
                        dve.wait_ge(phase_taken, phases + source + 1)
                    if u.layer == 0:
                        no = halves_before(section, u.phase, j)
                        if u.t == 0:
                            dve.wait_ge(pair_rep_loaded, (no + 1) * 16)
                        r = u.t % PAIR_RING
                        per_half = len(range(r, UNITS_0, PAIR_RING))
                        dve.wait_ge(shift_loaded[r], (no * per_half + u.t // PAIR_RING + 1) * 16)
                        in0, in1 = pair_rep[:], pair_shift[:, r, :]
                    else:
                        if u.layer == 1:
                            no = halves_before(section, u.phase, j)
                            dve.wait_ge(x0_rep_loaded[u.t], (no + 1) * (16 * (u.rows // KEPT)))
                        in0, in1 = (x1, x2)[u.layer - 1][0:u.rows, :], x0_rep[0:u.rows, u.t, :]
                    old = section.before(u, section.p_slot, lambda x: True)
                    if old is not None:
                        if old.split:
                            dve.wait_ge(lo_ready, splits + old.s + 1)
                        else:
                            dve.wait_ge(unit_done, units + old.n + 1)
                    nc.vector.tensor_tensor(prod[0:u.rows, section.p_slot(u), :], in0, in1,
                                            ALU.mult).then_inc(prod_ready, 1)
                    if u.split:
                        waiting.append(u)
                    if waiting and waiting[0].n == u.n - LAG:
                        low_part(section, waiting.pop(0), units, splits)
                    for args in events.get((u.phase, u.t), ()):
                        reduce_half(*args)
                assert not waiting

            section_products(None, FIRST, {})

            def loop_events(j, section):
                phases = counts_before(section, j)[2]
                ev = {(0, 5): [(j, 1, 0, A, phases)],
                      (2, 6): [(j, 2, 1, A, phases + 2)],
                      (3, 5): [(j, 3, 0, B, phases + 3)]}
                if section is LOOP:
                    ev[(5, 6)] = [(j, 4, 1, B, phases + 5)]
                return ev

            with dve.Fori(0, BLOCKS - 1) as j:
                section_products(j, LOOP, loop_events(j, LOOP))
            j = BLOCKS - 1
            section_products(j, LAST, loop_events(j, LAST))
            reduce_half(j, 4, 1, B, counts_before(LAST, j)[2] + 4)

        @block.scalar
        def _(act):
            def take_turned(j, g):
                n = j * TURNS + g
                act.wait_ge(turned_ready, n + 1)
                nc.scalar.copy(x0_sb[:, g * BANK:(g + 1) * BANK],
                               turned[0:2 * FIELDS, g, :]).then_inc(turned_taken, 1)

            def take_phase(section, ph, units):
                layer = section.phases[ph][0] if ph >= 0 else 1
                end = section.at(ph, UNITS[layer] - 1) + 1 if ph >= 0 else 0
                slot = ph % 2
                act.wait_ge(unit_done, units + end)
                z, b = acc[:, slot, :], bias_sb[:, layer:layer + 1]
                relu = ACT.Relu
                if layer == 0:
                    nc.scalar.activation(x1[0:KEPT, :], z[0:KEPT, :], relu, bias=b[0:KEPT, :])
                    nc.scalar.activation(x1[KEPT:128, :], z[0:KEPT, :], relu, bias=b[0:KEPT, :])
                    nc.scalar.activation(direct01[KEPT:128, :], z[KEPT:128, :], relu,
                                                bias=b[KEPT:128, :]).then_inc(phase_taken, 1)
                if layer == 1:
                    nc.scalar.activation(x2[0:KEPT, :], z[KEPT:128, :], relu, bias=b[KEPT:128, :])
                    nc.scalar.activation(x2[KEPT:128, :], z[KEPT:128, :], relu, bias=b[KEPT:128, :])
                    nc.scalar.activation(direct01[0:KEPT, :], z[0:KEPT, :], relu,
                                                bias=b[0:KEPT, :]).then_inc(phase_taken, 1)
                if layer == 2:
                    nc.scalar.activation(direct2[:], z, relu, bias=b).then_inc(phase_taken, 1)

            def top_relu1(j):
                act.wait_ge(top1_done, j + 1)
                for m in range(TOP1 // 128):
                    last = nc.scalar.activation(h1[:, m, :], top_a[:, m, :], ACT.Relu, bias=tb1_sb[:, m:m + 1])
                last.then_inc(h1_ready, 1)

            def top_relu2(j):
                act.wait_ge(top2_done, j + 1)
                for m in range(TOP2 // 128):
                    last = nc.scalar.activation(h2[:, m, :], top_b[:, m, :], ACT.Relu, bias=tb2_sb[:, m:m + 1])
                last.then_inc(h2_ready, 1)

            def store_y(j):
                act.wait_ge(top3_done, j + 1)
                nc.scalar.copy(y_sb[:], top_b[0:1, TOP2 // 128, :]).then_inc(y_ready, 1)
                act.wait_ge(y_ready, j + 1)
                act.dma_start(out_rows[bass.ds(j, 1), :], y_sb[:]).then_inc(y_stored, 16)

            def section_scalar(j, section, events):
                units, splits, phases = counts_before(section, j)
                for u in section.units:
                    if u.t == 0 and section.needs_last_phase(u.phase):
                        take_phase(section, u.phase - 1, units)
                    if u.split:
                        if (old := section.before(u, section.part_slot, lambda x: x.split)) is not None:
                            act.wait_ge(unit_done, units + old.n + 1)
                        act.wait_ge(prod_ready, units + u.n + 1)
                        nc.scalar.copy(prod_hi[0:u.rows, section.part_slot(u), :],
                                       prod[0:u.rows, section.p_slot(u), :]).then_inc(hi_ready, 1)
                    if u.t == EVAC_AT and not section.needs_last_phase(u.phase) and not (
                            section is FIRST and u.phase == 0):
                        take_phase(section, u.phase - 1, units)
                    for step in events.get((u.phase, u.t), ()):
                        step()

            act.wait_ge(consts_loaded, 16 * N_CONSTS)
            for g in range(TURNS):
                take_turned(0, g)
            section_scalar(None, FIRST, {})
            with act.Fori(0, BLOCKS - 1) as j:
                act.wait_ge(x0_stored, 32 * (j + 1))
                ev = {(0, g + 2): [lambda g=g: take_turned(j + 1, g)] for g in range(TURNS)}
                ev[(5, 11)] = [lambda: top_relu1(j)]
                ev[(5, 14)] = [lambda: top_relu2(j)]
                ev[(5, 17)] = [lambda: store_y(j)]
                section_scalar(j, LOOP, ev)
                act.wait_ge(y_stored, 16 * (j + 1))
            j = BLOCKS - 1
            section_scalar(j, LAST, {})
            take_phase(LAST, 3, counts_before(LAST, j)[0])
            top_relu1(j)
            top_relu2(j)
            store_y(j)
            act.wait_ge(y_stored, 16 * BLOCKS)

        @block.tensor
        def _(pe):
            emb_by_dim = emb[:].rearrange("p (r q) -> p q r", q=DIM // 2)

            def turn(j, g, first=False):
                if g == 0:
                    pe.wait_ge(gathered, (j + 1) * (16 * FIELDS))
                if not first:
                    pe.wait_ge(turned_taken, j * TURNS + (g - 1))
                for q in range(4):
                    last = nc.tensor.transpose(turned[0:2 * FIELDS, g, q * ROWS:(q + 1) * ROWS],
                                               emb_by_dim[:, 4 * g + q, :], eye_sb[:])
                last.then_inc(turned_ready, 1)

            def top_layer1(j):
                pe.wait_ge(sums_ready, 2 * (j + 1))
                pe.wait_ge(context_loaded, 16 * (j + 1))
                for m in range(TOP1 // 128):
                    cols = slice(m * 128, (m + 1) * 128)
                    nc.tensor.matmul(top_a[:, m, :], top1_sb[:, 0, cols], sums[:, 0, :], start=True, stop=False)
                    nc.tensor.matmul(top_a[:, m, :], top1_sb[:, 1, cols], sums[:, 1, :], start=False, stop=False)
                    last = nc.tensor.matmul(top_a[:, m, :], top1c_sb[:, cols], context_sb[:],
                                            start=False, stop=True)
                last.then_inc(top1_done, 1)

            def top_layer2(j):
                pe.wait_ge(h1_ready, j + 1)
                for m in range(TOP2 // 128):
                    for k in range(TOP1 // 128):
                        last = nc.tensor.matmul(top_b[:, m, :], top2_sb[:, k, m * 128:(m + 1) * 128],
                                                h1[:, k, :], start=k == 0, stop=k == TOP1 // 128 - 1)
                last.then_inc(top2_done, 1)

            def top_layer3(j):
                pe.wait_ge(h2_ready, j + 1)
                for k in range(TOP2 // 128):
                    last = nc.tensor.matmul(top_b[0:1, TOP2 // 128, :], top3_sb[:, k:k + 1], h2[:, k, :],
                                            start=k == 0, stop=k == TOP2 // 128 - 1)
                last.then_inc(top3_done, 1)

            def section_matmuls(j, section, events):
                units, splits, phases = counts_before(section, j)
                for u in section.units:
                    if u.t == 0 and not (section is FIRST):
                        pe.wait_ge(phase_taken, phases + (u.phase - 1))
                    first, last_unit = u.t == 0, u.t == UNITS[u.layer] - 1
                    slot = u.phase % 2
                    if u.split:
                        k = split_list.index((u.layer, u.t))
                        pe.wait_ge(lo_ready, splits + u.s + 1)
                        steps = [(w_hi[0:u.rows, k, :], prod_hi), (w_hi[0:u.rows, k, :], prod_lo),
                                 (w_lo[0:u.rows, k, :], prod_hi)]
                        ring = section.part_slot(u)
                    else:
                        k = whole_list.index((u.layer, u.t))
                        pe.wait_ge(prod_ready, units + u.n + 1)
                        steps = [(w_whole[0:u.rows, k, :], prod)]
                        ring = section.p_slot(u)
                    for i, (w, p) in enumerate(steps):
                        for c in range(HALF // BANK):
                            cols = slice(c * BANK, (c + 1) * BANK)
                            last = nc.tensor.matmul(acc[:, slot, cols], w, p[0:u.rows, ring, cols],
                                                    start=first and i == 0,
                                                    stop=last_unit and i == len(steps) - 1)
                    last.then_inc(unit_done, 1)
                    for step in events.get((u.phase, u.t), ()):
                        step()

            pe.wait_ge(consts_loaded, 16 * N_CONSTS)
            for g in range(TURNS):
                turn(0, g, first=True)
            pe.wait_ge(weights_ready, 1)
            section_matmuls(None, FIRST, {})
            with pe.Fori(0, BLOCKS - 1) as j:
                ev = {(0, g + 1): [lambda g=g: turn(j + 1, g)] for g in range(TURNS)}
                ev[(5, 9)] = [lambda: top_layer1(j)]
                ev[(5, 13)] = [lambda: top_layer2(j)]
                ev[(5, 16)] = [lambda: top_layer3(j)]
                section_matmuls(j, LOOP, ev)
            j = BLOCKS - 1
            section_matmuls(j, LAST, {})
            top_layer1(j)
            top_layer2(j)
            top_layer3(j)


def pair_indices():
    none = FIELDS * FIELDS
    one = np.full((UNITS_0, PAIR_ROWS), none)
    other = one.copy()
    for t in range(UNITS_0):
        for i in range(FIELDS):
            for r in range(PER_UNIT):
                shift = PER_UNIT * t + r
                k = (i + shift) % FIELDS
                if shift < SHIFTS:
                    one[t, PER_UNIT * i + r] = FIELDS * i + k
                    if shift > 0:
                        other[t, PER_UNIT * i + r] = FIELDS * k + i
    return one, other


def kernel(**inputs):
    import concourse.bacc as bacc
    from concourse.bass_utils import run_bass_kernel_spmd

    a = {name: np.asarray(value) for name, value in inputs.items()}
    one, other = pair_indices()
    flat0 = np.concatenate([a["L0_rec_w0"].reshape(FIELDS * FIELDS, SIZE), np.zeros((1, SIZE), np.float32)])
    w1 = a["L0_rec_w1"].reshape(FIELDS * KEPT, SIZE)
    b1 = a["L0_rec_b1"]
    top1 = a["W_top1"]
    arrays = {
        "ids": a["ids"],
        **{f"tbl_{f}": a[f"tbl_{f}"] for f in range(FIELDS)},
        "w0": flat0[one],
        "w0_mirror": flat0[other],
        "w1": np.concatenate([w1[:, KEPT:], w1[:, :KEPT]], axis=1),
        "w2": a["L0_rec_w2"].reshape(FIELDS * KEPT, SIZE),
        "bias0": a["L0_rec_b0"].reshape(SIZE, 1),
        "bias1": np.concatenate([b1[KEPT:], b1[:KEPT]]).reshape(SIZE, 1),
        "bias2": a["L0_rec_b2"].reshape(SIZE, 1),
        "top1": np.stack([np.concatenate([top1[KEPT:2 * KEPT], top1[:KEPT]]),
                          top1[2 * KEPT:4 * KEPT]], axis=1),
        "top1_context": top1[4 * KEPT:],
        "top2": a["W_top2"].reshape(TOP1 // 128, 128, TOP2).transpose(1, 0, 2),
        "top3": a["W_top3"].reshape(TOP2 // 128, 128).T,
        "top_bias1": a["b_top1"].reshape(TOP1 // 128, 128).T,
        "top_bias2": a["b_top2"].reshape(TOP2 // 128, 128).T,
        "context": a["dense_ctx"].reshape(BLOCKS, ROWS, CONTEXT).transpose(0, 2, 1),
        "eye": np.eye(128, dtype=np.float32),
    }
    arrays = {name: np.ascontiguousarray(x) for name, x in arrays.items()}
    nc = bacc.Bacc("TRN2", target_bir_lowering=False, num_devices=1)
    aps = {name: nc.dram_tensor(name, x.shape, mybir.dt.from_np(x.dtype), kind="ExternalInput").ap()
           for name, x in arrays.items()}
    out = nc.dram_tensor("y", (BATCH, 1), mybir.dt.float32, kind="ExternalOutput").ap()
    tables = [aps.pop(f"tbl_{f}") for f in range(FIELDS)]
    build(nc, aps.pop("ids"), tables, **aps, out=out)
    result = run_bass_kernel_spmd(nc, [arrays], core_ids=[0])
    return result.results[0]["y"]
```

```python
from contextlib import ExitStack

import numpy as np

import concourse.bass as bass
from concourse import mybir

FIELDS, DIM, BATCH = 39, 16, 2048
SIZE = 128
KEPT = SIZE // 2
ROWS = 128
BLOCKS = BATCH // ROWS
HALF = DIM // 2 * ROWS
BLOCK_COLS = DIM * ROWS
BANK = 512
SHIFTS = FIELDS // 2 + 1
SHORT_0, LAST_0 = 3, 6
FIRST_SHIFT = {0: 0, 1: 4, 2: 8, 4: 12, 5: 16}
SHORT_K = 10
CONTEXT, TOP1, TOP2 = 16, 512, 256

SPLIT = {0: (SHORT_0,), 1: (0, 4, 7, SHORT_K, 13, 15, 18), 2: (0, 4, 7, SHORT_K, 13, 15, 18)}
LOADS = [(0, 1), (2, 3), (4, 5), (6, 7), (8, 9), (SHORT_K,), (19,), (11, 12), (13, 14), (15, 16), (17, 18)]
GROUPS = {0: [(0,), (1,), (2,), (4,), (5,), (SHORT_0,), (LAST_0,)]}
for layer in (1, 2):
    GROUPS[layer] = [group for load in LOADS
                     for group in ([(t,) for t in load] if set(load) & set(SPLIT[layer]) else [load])]
UNITS = {layer: sum(map(len, groups)) for layer, groups in GROUPS.items()}
UNITS_0, UNITS_K = UNITS[0], UNITS[1]
OWN_LAST, IN_X1 = LAST_0 + 1, 5
PAIR_SLOT = {0: 0, 1: 1, 2: 2, 4: 3, SHORT_0: 0, LAST_0: 1, OWN_LAST: 2}
RELOADED = {SHORT_0: 0, LAST_0: 1, OWN_LAST: 2}
PAIR_SLOTS = 4
P_RING, PART_RING = 6, 2
LAG = 1
KEPT_AT, RESULTS_AT = 3, 4


def rows_of(layer, t):
    if t == (SHORT_0 if layer == 0 else SHORT_K):
        return 32 if layer == 0 else 64
    return 128


def first_field(t):
    return 2 * t - (t > SHORT_K)


class Unit:
    def __init__(self, layer, t, phase, i, n, s, g, place):
        self.layer, self.t, self.phase = layer, t, phase
        self.i, self.n, self.g = i, n, g
        self.s = s
        self.place = place
        self.rows = rows_of(layer, t)
        self.split = t in SPLIT[layer]


class Section:

    def __init__(self, phases, last=False, first=False):
        self.phases, self.first = phases, first
        self.units, self.groups = [], []
        place = s = 0
        for ph, (layer, half) in enumerate(phases):
            i = 0
            for group in GROUPS[layer]:
                made = []
                for t in group:
                    made.append(Unit(layer, t, ph, i, len(self.units), s, len(self.groups), place))
                    self.units.append(made[-1])
                    i, s, place = i + 1, s + made[-1].split, place + 1
                self.groups.append(made)
            place += place % 2
        self.splits = s
        self.place_shift = 0 if last else -place % P_RING
        self.s_shift = 0 if last else -s % PART_RING
        self.tail = []
        if not first:
            last_1 = Section([(1, A)], first=True)
            for u in last_1.units:
                self.tail.append(Unit(1, u.t, -1, u.i, u.n - len(last_1.units), u.s - last_1.splits,
                                      u.g - len(last_1.groups), u.place - len(last_1.units)))

    def unit(self, phase, t):
        return next(u for u in self.units if u.phase == phase and u.t == t)

    def begins(self, phase):
        u = next(u for u in self.units if u.phase == phase)
        return u.n, u.g

    def ends(self, phase):
        return 0 if phase < 0 else max(u.n for u in self.units if u.phase == phase) + 1

    def needs_last_phase(self, phase):
        if phase == 0:
            return False
        layer, half = self.phases[phase]
        return self.phases[phase - 1] == (layer - 1, half)

    def p_slot(self, u):
        return (u.place + (self.place_shift if u.n >= 0 else 0)) % P_RING

    def part_slot(self, u):
        return (u.s + (self.s_shift if u.n >= 0 else 0)) % PART_RING

    def before(self, u, slot, chosen):
        same = [x for x in self.tail + self.units if x.n < u.n and chosen(x) and slot(x) == slot(u)]
        return same[-1] if same else None


A, B = 0, 1
FIRST = Section([(0, A), (1, A)], first=True)
LOOP = Section([(0, B), (2, A), (1, B), (0, A), (2, B), (1, A)])
LAST = Section([(0, B), (2, A), (1, B), (2, B)], last=True)
assert LOOP.place_shift == 0 and LOOP.s_shift == 0, "the loop's sections must begin alike"


class Counts:

    def __init__(self, section, j):
        def so_far(of):
            return 0 if section is FIRST else j * of(LOOP) + of(FIRST)
        self.units = so_far(lambda x: len(x.units))
        self.groups = so_far(lambda x: len(x.groups))
        self.splits = so_far(lambda x: x.splits)
        self.phases = so_far(lambda x: len(x.phases))
        self.kept = so_far(lambda x: sum(layer < 2 for layer, _ in x.phases))


def halves_before(section, phase, j):
    if section is FIRST:
        return 0
    return j * 2 + (1 if section.phases[phase][1] == B else 2)


def build(nc, ids, tables, w0, w0_mirror, w12_whole, w12_split, bias0, bias1, bias2,
          top1, top1_context, top2, top3, top_bias1, top_bias2, context, eye, out):
    f32, f32r, i32, u32 = mybir.dt.float32, mybir.dt.float32r, mybir.dt.int32, mybir.dt.uint32
    ALU, ACT, AX = mybir.AluOpType, mybir.ActivationFunctionType, mybir.AxisListType

    whole_list = [(l, t) for l in UNITS for t in range(UNITS[l]) if t not in SPLIT[l]]
    split_list = [(l, t) for l in UNITS for t in range(UNITS[l]) if t in SPLIT[l]]
    whole_0 = sum(l == 0 for l, t in whole_list)
    split_0 = sum(l == 0 for l, t in split_list)
    out_rows = out.rearrange("(a b) c -> a (b c)", b=ROWS)

    x0_dram = nc.dram_tensor("x0_dram", [BLOCKS, 2 * FIELDS, BLOCK_COLS], f32)

    with ExitStack() as ctx:
        def sb(name, shape, dtype=f32):
            return ctx.enter_context(nc.sbuf_tensor(name, shape, dtype))

        def sem(name):
            return ctx.enter_context(nc.semaphore(name))

        x0_rep = sb("x0_rep", [128, UNITS_K, HALF])
        pair_rep = sb("pair_rep", [128, HALF])
        pair_shift = sb("pair_shift", [128, PAIR_SLOTS, HALF])
        x1 = sb("x1", [128, HALF])
        x2 = sb("x2", [128, HALF])
        direct01 = sb("direct01", [128, HALF])
        direct2 = sb("direct2", [128, HALF])
        x0_sb = direct2[0:2 * FIELDS, :]
        prod = sb("prod", [128, P_RING, HALF])
        prod_hi = sb("prod_hi", [128, PART_RING, HALF], f32r)
        prod_lo = sb("prod_lo", [128, PART_RING, HALF], f32r)
        w_whole = sb("w_whole", [128, len(whole_list), SIZE])
        w_hi = sb("w_hi", [128, len(split_list), SIZE], f32r)
        w_lo = sb("w_lo", [128, len(split_list), SIZE], f32r)
        ids_sb = sb("ids_sb", [ROWS, FIELDS], i32)
        emb = sb("emb", [ROWS, FIELDS * DIM])
        sums = sb("sums", [128, 2, ROWS])
        part_sums = sb("part_sums", [128, 2, ROWS])
        context_sb = sb("context_sb", [CONTEXT, ROWS])
        top1_sb = sb("top1_sb", [128, 2, TOP1])
        top1c_sb = sb("top1c_sb", [CONTEXT, TOP1])
        top2_sb = sb("top2_sb", [128, TOP1 // 128, TOP2])
        top3_sb = sb("top3_sb", [128, TOP2 // 128])
        tb1_sb = sb("tb1_sb", [128, TOP1 // 128])
        tb2_sb = sb("tb2_sb", [128, TOP2 // 128])
        bias_sb = sb("bias_sb", [128, 3])
        h1 = sb("h1", [128, TOP1 // 128, ROWS])
        h2 = sb("h2", [128, TOP2 // 128, ROWS])
        y_sb = sb("y_sb", [1, ROWS])
        eye_sb = sb("eye_sb", [128, 128])

        acc = ctx.enter_context(nc.psum_tensor("acc", [128, 2, HALF], f32))
        turned = ctx.enter_context(nc.psum_tensor("turned", [128, 2, BANK], f32))
        top_a = ctx.enter_context(nc.psum_tensor("top_a", [128, TOP1 // 128, ROWS], f32))
        top_b = ctx.enter_context(nc.psum_tensor("top_b", [128, TOP1 // 128, ROWS], f32))

        raw = x0_rep[:, :, 0:SIZE]
        raw_direct = x0_rep[:, :, SIZE:2 * SIZE]
        raw_mirror = x0_rep[:, :, 2 * SIZE:3 * SIZE]
        SHORT_AT = slice(64, 96)
        pair_short = x0_rep[SHORT_AT, SHORT_K, :]

        consts_loaded = sem("consts_loaded")
        cin_weights_loaded = sem("cin_weights_loaded")
        pair_sums_ready = sem("pair_sums_ready")
        w_hi_ready = sem("w_hi_ready")
        weights_ready = sem("weights_ready")
        ids_loaded = sem("ids_loaded")
        gathered = sem("gathered")
        turned_ready = sem("turned_ready")
        turned_taken = sem("turned_taken")
        x0_stored = sem("x0_stored")
        pair_rep_loaded = sem("pair_rep_loaded")
        shift_loaded = [sem(f"shift_loaded{r}") for r in range(PAIR_SLOTS)]
        pair_x1_loaded = sem("pair_x1_loaded")
        pair_short_loaded = sem("pair_short_loaded")
        x0_rep_loaded = [sem(f"x0_rep_loaded{g}") for g in range(len(LOADS))]
        prod_ready = sem("prod_ready")
        hi_ready = sem("hi_ready")
        lo_ready = sem("lo_ready")
        unit_done = sem("unit_done")
        phase_taken = sem("phase_taken")
        half_reduced = sem("half_reduced")
        sums_ready = sem("sums_ready")
        context_loaded = sem("context_loaded")
        x_taken = sem("x_taken")
        stack_ready = sem("stack_ready")
        top1_done, top2_done, top3_done = sem("top1_done"), sem("top2_done"), sem("top3_done")
        h1_ready, h2_ready, y_ready = sem("h1_ready"), sem("h2_ready"), sem("y_ready")
        y_stored = sem("y_stored")
        waited, gather_waited = sem("waited"), sem("gather_waited")

        N_CONSTS = 10
        N_CIN = 4
        TURNS = HALF // BANK

        block = ctx.enter_context(nc.Block())

        @block.sync
        def _(sp):
            for dst, src in ((raw_direct[:, 0:UNITS_0, :], w0), (raw_mirror[:, 0:UNITS_0, :], w0_mirror),
                             (w_whole[:, whole_0:, :], w12_whole),
                             (raw[:, split_0:len(split_list), :], w12_split)):
                sp.dma_start(dst, src).then_inc(cin_weights_loaded, 16)

            def pairs_from(j, half, field, outer, inner):
                base = x0_dram[bass.ds(j, 1), field:field + 1, half * HALF:(half + 1) * HALF]
                return bass.AP(base.tensor, base.offset, [[outer[0] * BLOCK_COLS, outer[1]],
                                                          [inner[0] * BLOCK_COLS, inner[1]], [1, HALF]])

            def load_pair_slot(j, half, item, before):
                if before is not None:
                    sp.wait_ge(prod_ready, before)
                    sp.sem_inc(waited, 1)
                slot = x1[:] if item == IN_X1 else pair_shift[:, PAIR_SLOT[item], :]
                loaded = pair_x1_loaded if item == IN_X1 else shift_loaded[PAIR_SLOT[item]]
                if item in FIRST_SHIFT:
                    src = pairs_from(j, half, FIRST_SHIFT[item], (1, 32), (1, 4))
                elif item == SHORT_0:
                    slot, src = slot[SHORT_AT], pairs_from(j, half, 48, (1, 8), (1, 4))
                elif item == LAST_0:
                    src = pairs_from(j, half, 32, (1, 16), (1, 8))
                else:
                    src = pairs_from(j, half, 32, (0, 16), (1, 8))
                sp.dma_start(slot, src).then_inc(loaded, 16)

            def load_x0_rep(j, half, g, before):
                if before is not None:
                    sp.wait_ge(prod_ready, before)
                    sp.sem_inc(waited, 1)
                t, n = LOADS[g][0], len(LOADS[g])
                for r in range(rows_of(1, t) // KEPT):
                    sp.dma_start(x0_rep[r * KEPT:(r + 1) * KEPT, t:t + n, :],
                                 pairs_from(j, half, first_field(t) + r, (0, KEPT), (2, n))
                                 ).then_inc(x0_rep_loaded[g], 16)

            def store_x0(j):
                sp.wait_ge(turned_taken, TURNS * (j + 1))
                sp.sem_inc(waited, 1)
                for copy in (0, 1):
                    to = x0_dram[bass.ds(j, 1), copy * FIELDS:(copy + 1) * FIELDS, :]
                    sp.dma_start(to.rearrange("a f (h n) -> (a f h) n", h=2), x0_sb).then_inc(x0_stored, 16)
                sp.wait_ge(x0_stored, 32 * (j + 1))
                sp.sem_inc(waited, 1)

            def load_layer0(j, half, section, phase, section_j):
                groups, begin = Counts(section, section_j).groups, section.begins(phase)[1]
                before = None if section is FIRST else groups + begin - min(len(GROUPS[1]), len(GROUPS[2]))
                if before is not None:
                    sp.wait_ge(prod_ready, before)
                    sp.sem_inc(waited, 1)
                sp.dma_start(pair_rep[:], pairs_from(j, half, 0, (1, 32), (0, 4))).then_inc(pair_rep_loaded, 16)
                for item in (0, 1, 2, 4):
                    load_pair_slot(j, half, item, None)
                sp.dma_start(pair_short, pairs_from(j, half, 32, (1, 8), (0, 4))).then_inc(pair_short_loaded, 16)
                load_pair_slot(j, half, IN_X1, None if section is FIRST else groups + begin)
                for item, user in RELOADED.items():
                    load_pair_slot(j, half, item, groups + section.unit(phase, user).g + 1)

            for dst, src in ((eye_sb[:], eye), (bias_sb[:, 0:1], bias0), (bias_sb[:, 1:2], bias1),
                             (bias_sb[:, 2:3], bias2)):
                sp.dma_start(dst, src).then_inc(consts_loaded, 16)
            for dst, src in ((top1_sb[:], top1), (top1c_sb[:], top1_context), (top2_sb[:], top2),
                             (top3_sb[:], top3), (tb1_sb[:], top_bias1), (tb2_sb[:], top_bias2)):
                sp.dma_start(dst, src).then_inc(consts_loaded, 16)
            sp.dma_start(context_sb[:], context[0]).then_inc(context_loaded, 16)

            store_x0(0)
            sp.wait_ge(weights_ready, 1)
            load_layer0(0, A, FIRST, 0, None)
            for g in range(len(LOADS)):
                load_x0_rep(0, A, g, None)

            def section_loads(j, section):
                groups = Counts(section, j).groups
                load_layer0(j, B, section, 0, j)
                if section is LOOP:
                    store_x0(j + 1)
                for g, load in enumerate(LOADS):
                    load_x0_rep(j, B, g, groups + section.unit(1, load[-1]).g + 1)
                if section is LOOP:
                    load_layer0(j + 1, A, section, 3, j)
                    for g, load in enumerate(LOADS):
                        load_x0_rep(j + 1, A, g, groups + section.unit(4, load[-1]).g + 1)
                    sp.wait_ge(top1_done, j + 1)
                    sp.sem_inc(waited, 1)
                    sp.dma_start(context_sb[:], context[bass.ds(j + 1, 1)].rearrange("a p n -> (a p) n")
                                 ).then_inc(context_loaded, 16)

            with sp.Fori(0, BLOCKS - 1) as j:
                section_loads(j, LOOP)
            section_loads(BLOCKS - 1, LAST)

        @block.gpsimd
        def _(pool):
            def gather(j):
                pool.dma_start(ids_sb[:], ids[bass.ds(j * ROWS, ROWS), :]).then_inc(ids_loaded, 16)
                pool.wait_ge(ids_loaded, 16 * (j + 1))
                pool.sem_inc(gather_waited, 1)
                for f in range(FIELDS):
                    pool.indirect_dma_start(
                        out=emb[:, f * DIM:(f + 1) * DIM], out_offset=None, in_=tables[f],
                        in_offset=bass.IndirectOffsetOnAxis(ap=ids_sb[:, f:f + 1].bitcast(u32), axis=0),
                    ).then_inc(gathered, 16)

            gather(0)
            with pool.Fori(1, BLOCKS) as j:
                pool.wait_ge(gathered, 16 * FIELDS * j)
                pool.wait_ge(turned_ready, TURNS * j)
                gather(j)

        @block.vector
        def _(dve):
            dve.wait_ge(cin_weights_loaded, 16 * N_CIN)
            for t in range(UNITS_0):
                if (0, t) in whole_list:
                    to = w_whole[:, whole_list.index((0, t)), :]
                else:
                    to = raw[:, split_list.index((0, t)), :]
                nc.vector.tensor_tensor(to, raw_direct[:, t, :], raw_mirror[:, t, :],
                                        ALU.add).then_inc(pair_sums_ready, 1)
            dve.wait_ge(pair_sums_ready, UNITS_0)
            for k in range(len(split_list)):
                nc.vector.tensor_copy(w_hi[:, k, :], raw[:, k, :]).then_inc(w_hi_ready, 1)
            dve.wait_ge(w_hi_ready, len(split_list))
            for k, (l, t) in enumerate(split_list):
                at = SHORT_AT if (l, t) == (0, SHORT_0) else slice(0, rows_of(l, t))
                to = w_hi if (l, t) == (0, SHORT_0) else w_lo
                last = nc.vector.tensor_tensor(to[at, k, :], raw[at, k, :], w_hi[at, k, :].bitcast(f32),
                                               ALU.subtract)
            last.then_inc(weights_ready, 1)

            def low_part(section, u, before):
                if (old := section.before(u, section.part_slot, lambda x: x.split)) is not None:
                    dve.wait_ge(unit_done, before.units + old.n + 1)
                dve.wait_ge(prod_ready, before.groups + u.g + 1)
                dve.wait_ge(hi_ready, before.splits + u.s + 1)
                ring = section.part_slot(u)
                at, lo = slice(0, u.rows), prod_lo[:, ring, :]
                if u.rows == 64:
                    lo = prod_hi[64:128, ring, :]
                elif u.rows == 32:
                    at, lo = SHORT_AT, prod_hi[32:64, ring, :]
                nc.vector.tensor_tensor(lo, prod[at, section.p_slot(u), :], prod_hi[at, ring, :].bitcast(f32),
                                        ALU.subtract).then_inc(lo_ready, 1)

            def reduce_half(j, n, which, half, phase_no):
                src = (direct01, direct2)[which]
                dst = (sums, part_sums)[half]
                dve.wait_ge(phase_taken, phase_no)
                nc.vector.tensor_reduce(dst[:, which, :], src[:].rearrange("p (d b) -> p b d", b=ROWS),
                                        AX.X, ALU.add).then_inc(half_reduced, 1)
                if half == B:
                    dve.wait_ge(half_reduced, j * 4 + n)
                    nc.vector.tensor_tensor(sums[:, which, :], sums[:, which, :],
                                            part_sums[:, which, :], ALU.add).then_inc(sums_ready, 1)

            def section_products(j, section, events):
                before = Counts(section, j)
                waiting = []
                for group in section.groups:
                    u, n = group[0], len(group)
                    first_slot = section.p_slot(u)
                    to = prod[:, first_slot:first_slot + n, :]
                    no = halves_before(section, u.phase, j)
                    if u.i == 0 and section.needs_last_phase(u.phase):
                        while waiting:
                            low_part(section, waiting.pop(0), before)
                    if u.i == 0 and u.layer > 0:
                        half = section.phases[u.phase][1]
                        source = next((p for p in reversed(range(u.phase))
                                       if section.phases[p] == (u.layer - 1, half)), -1)
                        kept = sum(section.phases[p][0] < 2 for p in range(source + 1))
                        dve.wait_ge(x_taken, before.kept + kept)
                    if u.layer == 0:
                        if u.i == 0:
                            dve.wait_ge(pair_rep_loaded, (no + 1) * 16)
                        for item in (LAST_0, OWN_LAST) if u.t == LAST_0 else [x.t for x in group]:
                            if item == IN_X1:
                                dve.wait_ge(pair_x1_loaded, (no + 1) * 16)
                                continue
                            slot = PAIR_SLOT[item]
                            loads = list(PAIR_SLOT.values()).count(slot)
                            dve.wait_ge(shift_loaded[slot], (no * loads + (item in RELOADED) + 1) * 16)
                        slot = PAIR_SLOT.get(u.t, 0)
                        shifted = pair_shift[:, slot:slot + n, :]
                        own = pair_rep[:].unsqueeze(1).to_broadcast([128, n, HALF])
                        if u.t == IN_X1:
                            shifted = x1[:].unsqueeze(1)
                        elif u.t == SHORT_0:
                            dve.wait_ge(pair_short_loaded, (no + 1) * 16)
                            to, own, shifted = to[SHORT_AT, 0, :], pair_short, shifted[SHORT_AT, 0, :]
                        elif u.t == LAST_0:
                            own = pair_shift[:, PAIR_SLOT[OWN_LAST]:PAIR_SLOT[OWN_LAST] + 1, :]
                        operands = own, shifted
                    else:
                        if u.layer == 1:
                            g = next(g for g, load in enumerate(LOADS) if u.t in load)
                            dve.wait_ge(x0_rep_loaded[g], (no + 1) * (16 * (u.rows // KEPT)))
                        at = slice(0, u.rows)
                        to = to[at]
                        x = (x1, x2)[u.layer - 1][at, :].unsqueeze(1).to_broadcast([u.rows, n, HALF])
                        operands = x, x0_rep[at, u.t:u.t + n, :]
                    olds = [section.before(x, section.p_slot, lambda x: True) for x in group]
                    whole = [x.n for x in olds if x is not None and not x.split]
                    split = [x.s for x in olds if x is not None and x.split]
                    if whole:
                        dve.wait_ge(unit_done, before.units + max(whole) + 1)
                    if split:
                        dve.wait_ge(lo_ready, before.splits + max(split) + 1)
                    nc.vector.tensor_tensor(to, *operands, ALU.mult).then_inc(prod_ready, 1)
                    while waiting and waiting[0].g <= u.g - LAG:
                        low_part(section, waiting.pop(0), before)
                    waiting += [x for x in group if x.split]
                    for x in group:
                        for args in events.get((x.phase, x.i), ()):
                            reduce_half(*args)
                for u in waiting:
                    low_part(section, u, before)

            section_products(None, FIRST, {})

            def loop_events(j, section):
                phases = Counts(section, j).phases
                ev = {(0, 6): [(j, 1, 0, A, phases)],
                      (2, 6): [(j, 2, 1, A, phases + 2)],
                      (3, 6): [(j, 3, 0, B, phases + 3)]}
                if section is LOOP:
                    ev[(5, 6)] = [(j, 4, 1, B, phases + 5)]
                return ev

            with dve.Fori(0, BLOCKS - 1) as j:
                section_products(j, LOOP, loop_events(j, LOOP))
            j = BLOCKS - 1
            section_products(j, LAST, loop_events(j, LAST))
            reduce_half(j, 4, 1, B, Counts(LAST, j).phases + 4)

        @block.scalar
        def _(act):
            def take_turned(j, g):
                n = j * TURNS + g
                act.wait_ge(turned_ready, n + 1)
                nc.scalar.copy(x0_sb[:, g * BANK:(g + 1) * BANK],
                               turned[0:2 * FIELDS, g, :]).then_inc(turned_taken, 1)

            def last_phase(section, ph):
                layer = section.phases[ph][0] if ph >= 0 else 1
                return layer, acc[:, ph % 2, :], bias_sb[:, layer:layer + 1]

            def take_kept(section, ph, units):
                layer, z, b = last_phase(section, ph)
                act.wait_ge(unit_done, units + section.ends(ph))
                if layer < 2:
                    x, kept = ((x1, slice(0, KEPT)), (x2, slice(KEPT, 128)))[layer]
                    nc.scalar.activation(x[0:KEPT, :], z[kept, :], ACT.Relu, bias=b[kept, :])
                    nc.scalar.activation(x[KEPT:128, :], z[kept, :], ACT.Relu,
                                         bias=b[kept, :]).then_inc(x_taken, 1)

            def take_results(section, ph, j):
                layer, z, b = last_phase(section, ph)
                if layer == 0 and section is not FIRST:
                    n = 1 if section.phases[ph][1] == B else 3
                    act.wait_ge(half_reduced, j * 4 + n)
                if layer == 2 and section is LOOP:
                    act.wait_ge(x0_stored, 32 * (j + 2))
                at = (slice(KEPT, 128), slice(0, KEPT), slice(0, 128))[layer]
                to = direct2 if layer == 2 else direct01
                nc.scalar.activation(to[at, :], z[at, :], ACT.Relu, bias=b[at, :]).then_inc(phase_taken, 1)

            def top_relu1(j):
                act.wait_ge(top1_done, j + 1)
                for m in range(TOP1 // 128):
                    last = nc.scalar.activation(h1[:, m, :], top_a[:, m, :], ACT.Relu, bias=tb1_sb[:, m:m + 1])
                last.then_inc(h1_ready, 1)

            def top_relu2(j):
                act.wait_ge(top2_done, j + 1)
                for m in range(TOP2 // 128):
                    last = nc.scalar.activation(h2[:, m, :], top_b[:, m, :], ACT.Relu, bias=tb2_sb[:, m:m + 1])
                last.then_inc(h2_ready, 1)

            def store_y(j):
                act.wait_ge(top3_done, j + 1)
                nc.scalar.copy(y_sb[:], top_b[0:1, TOP2 // 128, :]).then_inc(y_ready, 1)
                act.wait_ge(y_ready, j + 1)
                act.dma_start(out_rows[bass.ds(j, 1), :], y_sb[:]).then_inc(y_stored, 16)

            def section_scalar(j, section, events):
                before = Counts(section, j)
                units = before.units
                for u in section.units:
                    if u.i == 0 and section.needs_last_phase(u.phase):
                        take_kept(section, u.phase - 1, units)
                        take_results(section, u.phase - 1, j)
                    if u.split:
                        if (old := section.before(u, section.part_slot, lambda x: x.split)) is not None:
                            act.wait_ge(unit_done, units + old.n + 1)
                        act.wait_ge(prod_ready, before.groups + u.g + 1)
                        hi, p = prod_hi[:, section.part_slot(u), :], prod[:, section.p_slot(u), :]
                        at = SHORT_AT if u.rows == 32 else slice(0, u.rows)
                        nc.scalar.copy(hi[at, :], p[at, :]).then_inc(hi_ready, 1)
                        if u.rows == 32:
                            nc.scalar.copy(hi[0:32, :], p[at, :]).then_inc(stack_ready, 1)
                    if not section.needs_last_phase(u.phase) and not (section is FIRST and u.phase == 0):
                        if u.i == KEPT_AT:
                            take_kept(section, u.phase - 1, units)
                        if u.i == RESULTS_AT:
                            take_results(section, u.phase - 1, j)
                    for step in events.get((u.phase, u.i), ()):
                        step()

            act.wait_ge(consts_loaded, 16 * N_CONSTS)
            for g in range(TURNS):
                take_turned(0, g)
            section_scalar(None, FIRST, {})
            with act.Fori(0, BLOCKS - 1) as j:
                ev = {(0, 5 + g): [lambda g=g: take_turned(j + 1, g)] for g in range(TURNS)}
                ev[(5, 10)] = [lambda: top_relu1(j)]
                ev[(5, 14)] = [lambda: top_relu2(j)]
                ev[(5, 17)] = [lambda: store_y(j)]
                section_scalar(j, LOOP, ev)
                act.wait_ge(y_stored, 16 * (j + 1))
            j = BLOCKS - 1
            section_scalar(j, LAST, {})
            take_kept(LAST, 3, Counts(LAST, j).units)
            take_results(LAST, 3, j)
            top_relu1(j)
            top_relu2(j)
            store_y(j)
            act.wait_ge(y_stored, 16 * BLOCKS)

        @block.tensor
        def _(pe):
            emb_by_dim = emb[:].rearrange("p (r q) -> p q r", q=DIM // 2)

            def turn(j, g, first=False):
                if g == 0:
                    pe.wait_ge(gathered, (j + 1) * (16 * FIELDS))
                if not first:
                    pe.wait_ge(turned_taken, j * TURNS + (g - 1))
                for q in range(4):
                    last = nc.tensor.transpose(turned[0:2 * FIELDS, g, q * ROWS:(q + 1) * ROWS],
                                               emb_by_dim[:, 4 * g + q, :], eye_sb[:])
                last.then_inc(turned_ready, 1)

            def top_layer1(j):
                pe.wait_ge(sums_ready, 2 * (j + 1))
                pe.wait_ge(context_loaded, 16 * (j + 1))
                for m in range(TOP1 // 128):
                    cols = slice(m * 128, (m + 1) * 128)
                    nc.tensor.matmul(top_a[:, m, :], top1_sb[:, 0, cols], sums[:, 0, :], start=True, stop=False)
                    nc.tensor.matmul(top_a[:, m, :], top1_sb[:, 1, cols], sums[:, 1, :], start=False, stop=False)
                    last = nc.tensor.matmul(top_a[:, m, :], top1c_sb[:, cols], context_sb[:],
                                            start=False, stop=True)
                last.then_inc(top1_done, 1)

            def top_layer2(j):
                pe.wait_ge(h1_ready, j + 1)
                for m in range(TOP2 // 128):
                    for k in range(TOP1 // 128):
                        last = nc.tensor.matmul(top_b[:, m, :], top2_sb[:, k, m * 128:(m + 1) * 128],
                                                h1[:, k, :], start=k == 0, stop=k == TOP1 // 128 - 1)
                last.then_inc(top2_done, 1)

            def top_layer3(j):
                pe.wait_ge(h2_ready, j + 1)
                for k in range(TOP2 // 128):
                    last = nc.tensor.matmul(top_b[0:1, TOP2 // 128, :], top3_sb[:, k:k + 1], h2[:, k, :],
                                            start=k == 0, stop=k == TOP2 // 128 - 1)
                last.then_inc(top3_done, 1)

            def section_matmuls(j, section, events):
                before = Counts(section, j)
                for u in section.units:
                    first, last_unit = u.i == 0, u.i == UNITS[u.layer] - 1
                    if first and section is not FIRST:
                        pe.wait_ge(phase_taken, before.phases + (u.phase - 1))
                    slot = u.phase % 2
                    if u.split:
                        k = split_list.index((u.layer, u.t))
                        pe.wait_ge(lo_ready, before.splits + u.s + 1)
                        if u.rows == 32:
                            pe.wait_ge(stack_ready, halves_before(section, u.phase, j) + 1)
                        steps = {128: [(w_hi, prod_hi, 128), (w_hi, prod_lo, 128), (w_lo, prod_hi, 128)],
                                 64: [(w_hi, prod_hi, 128), (w_lo, prod_hi, 64)],
                                 32: [(w_hi, prod_hi, 96)]}[u.rows]
                        ring = section.part_slot(u)
                    else:
                        k = whole_list.index((u.layer, u.t))
                        pe.wait_ge(prod_ready, before.groups + u.g + 1)
                        steps = [(w_whole, prod, 128)]
                        ring = section.p_slot(u)
                    for i, (w, p, rows) in enumerate(steps):
                        for c in range(HALF // BANK):
                            cols = slice(c * BANK, (c + 1) * BANK)
                            last = nc.tensor.matmul(acc[:, slot, cols], w[0:rows, k, :], p[0:rows, ring, cols],
                                                    start=first and i == 0,
                                                    stop=last_unit and i == len(steps) - 1)
                    last.then_inc(unit_done, 1)
                    for step in events.get((u.phase, u.i), ()):
                        step()

            pe.wait_ge(consts_loaded, 16 * N_CONSTS)
            for g in range(TURNS):
                turn(0, g, first=True)
            pe.wait_ge(weights_ready, 1)
            section_matmuls(None, FIRST, {})
            with pe.Fori(0, BLOCKS - 1) as j:
                ev = {(0, g): [lambda g=g: turn(j + 1, g)] for g in range(TURNS)}
                ev[(5, 5)] = [lambda: top_layer1(j)]
                ev[(5, 9)] = [lambda: top_layer2(j)]
                ev[(5, 13)] = [lambda: top_layer3(j)]
                section_matmuls(j, LOOP, ev)
            j = BLOCKS - 1
            section_matmuls(j, LAST, {})
            top_layer1(j)
            top_layer2(j)
            top_layer3(j)


def pair_indices():
    none = FIELDS * FIELDS
    one = np.full((128, UNITS_0), none)
    other = one.copy()

    def put(row, t, i, shift):
        k = (i + shift) % FIELDS
        if i < FIELDS:
            one[row, t] = FIELDS * i + k
            if shift > 0:
                other[row, t] = FIELDS * k + i

    for t, first in FIRST_SHIFT.items():
        for row in range(128):
            put(row, t, row // 4, first + row % 4)
    for row in range(128):
        put(row, LAST_0, 32 + row % 8, row // 8)
    for row in range(96):
        put(row, SHORT_0, 32 + row % 32 // 4, 16 + row % 4)
    return one, other


def unit_weights(w, t):
    rows = w[first_field(t) * KEPT:first_field(t) * KEPT + rows_of(1, t)]
    return np.concatenate([rows, rows]) if t == SHORT_K else rows


def kernel(**inputs):
    import concourse.bacc as bacc
    from concourse.bass_utils import run_bass_kernel_spmd

    a = {name: np.asarray(value) for name, value in inputs.items()}
    one, other = pair_indices()
    flat0 = np.concatenate([a["L0_rec_w0"].reshape(FIELDS * FIELDS, SIZE), np.zeros((1, SIZE), np.float32)])
    w1 = a["L0_rec_w1"].reshape(FIELDS * KEPT, SIZE)
    w12 = {1: np.concatenate([w1[:, KEPT:], w1[:, :KEPT]], axis=1),
           2: a["L0_rec_w2"].reshape(FIELDS * KEPT, SIZE)}
    b1 = a["L0_rec_b1"]
    top1 = a["W_top1"]
    arrays = {
        "ids": a["ids"],
        **{f"tbl_{f}": a[f"tbl_{f}"] for f in range(FIELDS)},
        "w0": flat0[one],
        "w0_mirror": flat0[other],
        "w12_whole": np.stack([unit_weights(w12[l], t) for l in (1, 2) for t in range(UNITS_K)
                               if t not in SPLIT[l]], axis=1),
        "w12_split": np.stack([unit_weights(w12[l], t) for l in (1, 2) for t in range(UNITS_K)
                               if t in SPLIT[l]], axis=1),
        "bias0": a["L0_rec_b0"].reshape(SIZE, 1),
        "bias1": np.concatenate([b1[KEPT:], b1[:KEPT]]).reshape(SIZE, 1),
        "bias2": a["L0_rec_b2"].reshape(SIZE, 1),
        "top1": np.stack([np.concatenate([top1[KEPT:2 * KEPT], top1[:KEPT]]),
                          top1[2 * KEPT:4 * KEPT]], axis=1),
        "top1_context": top1[4 * KEPT:],
        "top2": a["W_top2"].reshape(TOP1 // 128, 128, TOP2).transpose(1, 0, 2),
        "top3": a["W_top3"].reshape(TOP2 // 128, 128).T,
        "top_bias1": a["b_top1"].reshape(TOP1 // 128, 128).T,
        "top_bias2": a["b_top2"].reshape(TOP2 // 128, 128).T,
        "context": a["dense_ctx"].reshape(BLOCKS, ROWS, CONTEXT).transpose(0, 2, 1),
        "eye": np.eye(128, dtype=np.float32),
    }
    arrays = {name: np.ascontiguousarray(x) for name, x in arrays.items()}
    nc = bacc.Bacc("TRN2", target_bir_lowering=False, num_devices=1)
    aps = {name: nc.dram_tensor(name, x.shape, mybir.dt.from_np(x.dtype), kind="ExternalInput").ap()
           for name, x in arrays.items()}
    out = nc.dram_tensor("y", (BATCH, 1), mybir.dt.float32, kind="ExternalOutput").ap()
    tables = [aps.pop(f"tbl_{f}") for f in range(FIELDS)]
    build(nc, aps.pop("ids"), tables, **aps, out=out)
    result = run_bass_kernel_spmd(nc, [arrays], core_ids=[0])
    return result.results[0]["y"]
```

```python
from contextlib import ExitStack

import numpy as np

import concourse.bass as bass
from concourse import mybir

FIELDS, DIM, BATCH = 39, 16, 2048
SIZE = 128
KEPT = SIZE // 2
ROWS = 128
BLOCKS = BATCH // ROWS
HALF = DIM // 2 * ROWS
BLOCK_COLS = DIM * ROWS
BANK = 512
SHORT_0, LAST_0 = 3, 6
FIRST_SHIFT = {0: 0, 1: 4, 2: 8, 4: 12, 5: 16}
SHORT_K = 10
CONTEXT, TOP1, TOP2 = 16, 512, 256

SPLIT = {0: (1, 3), 1: (1, 2, 4, 6, 7, 9, 10, 11, 13, 14, 15, 18),
         2: (1, 2, 4, 7, 9, 10, 12, 13, 15, 17, 18, 19)}
LOADS = [(0, 1), (2, 3), (4, 5), (6, 7), (8, 9), (SHORT_K,), (19,), (11, 12), (13, 14), (15, 16), (17, 18)]
GROUPS = {0: [(0,), (1,), (2,), (4,), (5,), (SHORT_0,), (LAST_0,)]}
for layer in (1, 2):
    GROUPS[layer] = [group for load in LOADS
                     for group in ([(t,) for t in load] if set(load) & set(SPLIT[layer]) else [load])]
A, B = 0, 1
VECTOR_LOWS = {(0, A): (), (0, B): (1,), (1, A): (1, 2, 7, 11, 13, 15), (1, B): (7, 13, 14),
               (2, A): (4, 7, 13, 18), (2, B): (2, 7, 13, 18)}
UNITS = {layer: sum(map(len, groups)) for layer, groups in GROUPS.items()}
UNITS_0, UNITS_K = UNITS[0], UNITS[1]
OWN_LAST = LAST_0 + 1
PAIR_SLOT = {0: 0, 1: 1, 2: 2, 4: 3, 5: 4, SHORT_0: 0, LAST_0: 1, OWN_LAST: 2}
RELOADED = {SHORT_0: 0, LAST_0: 1, OWN_LAST: 2}
PAIR_SLOTS = 5
P_RING, HI_RING = 6, 4
LAG = 2
TURN_AT, GATHER_LAG = 5, 3
STORE_AT = 5
KEPT_AT, RESULTS_AT = 2, 3


def rows_of(layer, t):
    if t == (SHORT_0 if layer == 0 else SHORT_K):
        return 32 if layer == 0 else 64
    return 128


def first_field(t):
    return 2 * t - (t > SHORT_K)


class Unit:
    def __init__(self, layer, half, t, phase, i, n, s, g, place, pool_lows=0):
        self.layer, self.t, self.phase = layer, t, phase
        self.i, self.n, self.g = i, n, g
        self.s = s
        self.place = place
        self.rows = rows_of(layer, t)
        self.split = t in SPLIT[layer]
        self.low_by_pool = self.split and self.rows == 128 and t not in VECTOR_LOWS[layer, half]
        self.pool_lows = pool_lows


class Section:

    def __init__(self, phases, last=False, first=False):
        self.phases, self.first = phases, first
        self.units, self.groups = [], []
        place = s = pool_lows = 0
        for ph, (layer, half) in enumerate(phases):
            i = 0
            for group in GROUPS[layer]:
                made = []
                for t in group:
                    made.append(Unit(layer, half, t, ph, i, len(self.units), s, len(self.groups), place,
                                     pool_lows))
                    self.units.append(made[-1])
                    pool_lows += made[-1].low_by_pool
                    i, s, place = i + 1, s + made[-1].split, place + 1
                self.groups.append(made)
            place += place % 2
        self.splits, self.pool_lows = s, pool_lows
        self.place_shift = 0 if last else -place % P_RING
        self.s_shift = 0 if last else -s % HI_RING
        self.tail = []
        if not first:
            last_1 = Section([(1, A)], first=True)
            for u in last_1.units:
                self.tail.append(Unit(1, A, u.t, -1, u.i, u.n - len(last_1.units), u.s - last_1.splits,
                                      u.g - len(last_1.groups), u.place - len(last_1.units)))

    def unit(self, phase, t):
        return next(u for u in self.units if u.phase == phase and u.t == t)

    def begins(self, phase):
        u = next(u for u in self.units if u.phase == phase)
        return u.n, u.g

    def ends(self, phase):
        return 0 if phase < 0 else max(u.n for u in self.units if u.phase == phase) + 1

    def needs_last_phase(self, phase):
        if phase == 0:
            return False
        layer, half = self.phases[phase]
        return self.phases[phase - 1] == (layer - 1, half)

    def p_slot(self, u):
        return (u.place + (self.place_shift if u.n >= 0 else 0)) % P_RING

    def hi_slot(self, u):
        return (u.s + (self.s_shift if u.n >= 0 else 0)) % HI_RING

    def before(self, u, slot, chosen):
        same = [x for x in self.tail + self.units if x.n < u.n and chosen(x) and slot(x) == slot(u)]
        return same[-1] if same else None


FIRST = Section([(0, A), (1, A)], first=True)
LOOP = Section([(0, B), (2, A), (1, B), (0, A), (2, B), (1, A)])
LAST = Section([(0, B), (2, A), (1, B), (2, B)], last=True)
assert LOOP.place_shift == 0 and LOOP.s_shift == 0, "the loop's sections must begin alike"


class Counts:

    def __init__(self, section, j):
        def so_far(of):
            return 0 if section is FIRST else j * of(LOOP) + of(FIRST)
        self.units = so_far(lambda x: len(x.units))
        self.groups = so_far(lambda x: len(x.groups))
        self.splits = so_far(lambda x: x.splits)
        self.pool_lows = so_far(lambda x: x.pool_lows)
        self.vector_lows = so_far(lambda x: x.splits - x.pool_lows)
        self.phases = so_far(lambda x: len(x.phases))
        self.kept = so_far(lambda x: sum(layer < 2 for layer, _ in x.phases))


def halves_before(section, phase, j):
    if section is FIRST:
        return 0
    return j * 2 + (1 if section.phases[phase][1] == B else 2)


def build(nc, ids, tables, w0, w0_mirror, w12_whole, w12_split, bias0, bias1, bias2,
          top1, top1_context, top2, top3, top_bias1, top_bias2, context, eye, out):
    f32, f32r, i32, u32 = mybir.dt.float32, mybir.dt.float32r, mybir.dt.int32, mybir.dt.uint32
    ALU, ACT, AX = mybir.AluOpType, mybir.ActivationFunctionType, mybir.AxisListType

    whole_list = [(l, t) for l in UNITS for t in range(UNITS[l]) if t not in SPLIT[l]]
    split_list = [(l, t) for l in UNITS for t in range(UNITS[l]) if t in SPLIT[l]]
    whole_0 = sum(l == 0 for l, t in whole_list)
    split_0 = sum(l == 0 for l, t in split_list)
    out_rows = out.rearrange("(a b) c -> a b c", b=ROWS)

    x0_dram = nc.dram_tensor("x0_dram", [BLOCKS, 2 * FIELDS, BLOCK_COLS], f32)

    with ExitStack() as ctx:
        def sb(name, shape, dtype=f32):
            return ctx.enter_context(nc.sbuf_tensor(name, shape, dtype))

        def sem(name):
            return ctx.enter_context(nc.semaphore(name))

        x0_rep = sb("x0_rep", [128, UNITS_K, HALF])
        pair_rep = sb("pair_rep", [128, HALF])
        pair_shift = sb("pair_shift", [128, PAIR_SLOTS, HALF])
        direct01 = sb("direct01", [128, HALF])
        direct2 = sb("direct2", [128, HALF])
        x0_sb = direct2[0:2 * FIELDS, :]
        with nc.sbuf_tensor("prod", [128, P_RING, HALF], f32) as prod:
            pass
        prod_lo = sb("prod_lo", [128, P_RING, HALF], f32r)
        prod_hi = sb("prod_hi", [128, HI_RING, HALF], f32r)
        w_whole = sb("w_whole", [128, len(whole_list), SIZE])
        w_hi = sb("w_hi", [128, len(split_list), SIZE], f32r)
        w_lo = sb("w_lo", [128, len(split_list), SIZE], f32r)
        ids_sb = sb("ids_sb", [ROWS, FIELDS], i32)
        emb = sb("emb", [ROWS, FIELDS * DIM])
        sums = sb("sums", [128, 2, ROWS])
        part_sums = sb("part_sums", [128, 2, ROWS])
        context_sb = sb("context_sb", [CONTEXT, ROWS])
        top1_sb = sb("top1_sb", [128, 2, TOP1])
        top1c_sb = sb("top1c_sb", [CONTEXT, TOP1])
        top2_sb = sb("top2_sb", [128, TOP1 // 128, TOP2])
        top3_sb = sb("top3_sb", [128, TOP2 // 128])
        tb1_sb = sb("tb1_sb", [128, TOP1 // 128])
        tb2_sb = sb("tb2_sb", [128, TOP2 // 128])
        bias_sb = sb("bias_sb", [128, 3])
        h1 = direct2[:, 0:TOP1].rearrange("p (m n) -> p m n", n=ROWS)
        h2 = direct2[:, TOP1:TOP1 + TOP2].rearrange("p (m n) -> p m n", n=ROWS)
        y_sb = sb("y_sb", [ROWS, 1])
        eye_sb = sb("eye_sb", [128, 128])

        acc = ctx.enter_context(nc.psum_tensor("acc", [128, 2, HALF], f32))
        x1 = ctx.enter_context(nc.psum_tensor("x1", [128, HALF], f32))
        x2 = ctx.enter_context(nc.psum_tensor("x2", [128, HALF], f32))
        turned = acc[:, 0, :].rearrange("p (g n) -> p g n", n=BANK)
        top_a = acc[:, 0, 0:BANK].rearrange("p (m n) -> p m n", n=ROWS)
        top_b = acc[:, 0, BANK:HALF].rearrange("p (m n) -> p m n", n=ROWS)

        raw_slots = x0_rep[:].rearrange("p t (r c) -> p (t r) c", c=SIZE)
        raw = raw_slots[:, 0:len(split_list), :]
        raw_direct = raw_slots[:, len(split_list):len(split_list) + UNITS_0, :]
        raw_mirror = raw_slots[:, len(split_list) + UNITS_0:len(split_list) + 2 * UNITS_0, :]
        SHORT_AT = slice(64, 96)
        pair_short = x0_rep[SHORT_AT, SHORT_K, :]

        consts_loaded = sem("consts_loaded")
        cin_weights_loaded = sem("cin_weights_loaded")
        pair_sums_ready = sem("pair_sums_ready")
        w_hi_ready = sem("w_hi_ready")
        weights_ready = sem("weights_ready")
        ids_loaded = sem("ids_loaded")
        gathered = sem("gathered")
        turned_ready = sem("turned_ready")
        turned_taken = sem("turned_taken")
        x0_stored = sem("x0_stored")
        pair_rep_loaded = sem("pair_rep_loaded")
        shift_loaded = [sem(f"shift_loaded{r}") for r in range(PAIR_SLOTS)]
        pair_short_loaded = sem("pair_short_loaded")
        x0_rep_loaded = [sem(f"x0_rep_loaded{g}") for g in range(len(LOADS))]
        prod_ready = sem("prod_ready")
        hi_ready = sem("hi_ready")
        vector_lo_ready = sem("vector_lo_ready")
        pool_lo_ready = sem("pool_lo_ready")
        unit_done = sem("unit_done")
        phase_taken = sem("phase_taken")
        half_reduced = sem("half_reduced")
        sums_ready = sem("sums_ready")
        context_loaded = sem("context_loaded")
        x_taken = sem("x_taken")
        stack_ready = sem("stack_ready")
        top1_done, top2_done, top3_done = sem("top1_done"), sem("top2_done"), sem("top3_done")
        h1_ready, h2_ready, y_ready = sem("h1_ready"), sem("h2_ready"), sem("y_ready")
        y_stored = sem("y_stored")
        waited, pool_waited = sem("waited"), sem("pool_waited")

        N_CONSTS = 10
        N_CIN = 4
        TURNS = HALF // BANK

        block = ctx.enter_context(nc.Block())

        @block.sync
        def _(sp):
            for dst, src in ((raw_direct[:, 0:UNITS_0, :], w0), (raw_mirror[:, 0:UNITS_0, :], w0_mirror),
                             (w_whole[:, whole_0:, :], w12_whole),
                             (raw[:, split_0:len(split_list), :], w12_split)):
                sp.dma_start(dst, src).then_inc(cin_weights_loaded, 16)

            def pairs_from(j, half, field, outer, inner):
                base = x0_dram[bass.ds(j, 1), field:field + 1, half * HALF:(half + 1) * HALF]
                return bass.AP(base.tensor, base.offset, [[outer[0] * BLOCK_COLS, outer[1]],
                                                          [inner[0] * BLOCK_COLS, inner[1]], [1, HALF]])

            def load_pair_slot(j, half, item, before):
                if before is not None:
                    sp.wait_ge(prod_ready, before)
                    sp.sem_inc(waited, 1)
                slot, loaded = pair_shift[:, PAIR_SLOT[item], :], shift_loaded[PAIR_SLOT[item]]
                if item in FIRST_SHIFT:
                    src = pairs_from(j, half, FIRST_SHIFT[item], (1, 32), (1, 4))
                elif item == SHORT_0:
                    slot, src = slot[SHORT_AT], pairs_from(j, half, 48, (1, 8), (1, 4))
                elif item == LAST_0:
                    src = pairs_from(j, half, 32, (1, 16), (1, 8))
                else:
                    src = pairs_from(j, half, 32, (0, 16), (1, 8))
                sp.dma_start(slot, src).then_inc(loaded, 16)

            def load_x0_rep(j, half, g, before):
                if before is not None:
                    sp.wait_ge(prod_ready, before)
                    sp.sem_inc(waited, 1)
                t, n = LOADS[g][0], len(LOADS[g])
                for r in range(rows_of(1, t) // KEPT):
                    sp.dma_start(x0_rep[r * KEPT:(r + 1) * KEPT, t:t + n, :],
                                 pairs_from(j, half, first_field(t) + r, (0, KEPT), (2, n))
                                 ).then_inc(x0_rep_loaded[g], 16)

            def store_x0(j):
                sp.wait_ge(turned_taken, TURNS * (j + 1))
                sp.sem_inc(waited, 1)
                for copy in (0, 1):
                    to = x0_dram[bass.ds(j, 1), copy * FIELDS:(copy + 1) * FIELDS, :]
                    sp.dma_start(to.rearrange("a f (h n) -> (a f h) n", h=2), x0_sb).then_inc(x0_stored, 16)

            def load_layer0(j, half, section, phase, section_j):
                if section is FIRST or half == A:
                    sp.wait_ge(x0_stored, 32 * (j + 1))
                    sp.sem_inc(waited, 1)
                groups, begin = Counts(section, section_j).groups, section.begins(phase)[1]
                before = None if section is FIRST else groups + begin - min(len(GROUPS[1]), len(GROUPS[2]))
                if before is not None:
                    sp.wait_ge(prod_ready, before)
                    sp.sem_inc(waited, 1)
                sp.dma_start(pair_rep[:], pairs_from(j, half, 0, (1, 32), (0, 4))).then_inc(pair_rep_loaded, 16)
                for item in (0, 1, 2, 4, 5):
                    load_pair_slot(j, half, item, None)
                sp.dma_start(pair_short, pairs_from(j, half, 32, (1, 8), (0, 4))).then_inc(pair_short_loaded, 16)
                for item, user in RELOADED.items():
                    load_pair_slot(j, half, item, groups + section.unit(phase, user).g + 1)

            for dst, src in ((eye_sb[:], eye), (bias_sb[:, 0:1], bias0), (bias_sb[:, 1:2], bias1),
                             (bias_sb[:, 2:3], bias2)):
                sp.dma_start(dst, src).then_inc(consts_loaded, 16)
            for dst, src in ((top1_sb[:], top1), (top1c_sb[:], top1_context), (top2_sb[:], top2),
                             (top3_sb[:], top3), (tb1_sb[:], top_bias1), (tb2_sb[:], top_bias2)):
                sp.dma_start(dst, src).then_inc(consts_loaded, 16)
            sp.dma_start(context_sb[:], context[0]).then_inc(context_loaded, 16)

            store_x0(0)
            sp.wait_ge(weights_ready, 1)
            load_layer0(0, A, FIRST, 0, None)
            for g in range(len(LOADS)):
                load_x0_rep(0, A, g, None)

            def section_loads(j, section):
                groups = Counts(section, j).groups
                load_layer0(j, B, section, 0, j)
                for g, load in enumerate(LOADS):
                    if section is LOOP and g == STORE_AT:
                        store_x0(j + 1)
                    load_x0_rep(j, B, g, groups + section.unit(1, load[-1]).g + 1)
                if section is LOOP:
                    load_layer0(j + 1, A, section, 3, j)
                    for g, load in enumerate(LOADS):
                        load_x0_rep(j + 1, A, g, groups + section.unit(4, load[-1]).g + 1)
                    sp.wait_ge(top1_done, j + 1)
                    sp.sem_inc(waited, 1)
                    sp.dma_start(context_sb[:], context[bass.ds(j + 1, 1)].rearrange("a p n -> (a p) n")
                                 ).then_inc(context_loaded, 16)

            with sp.Fori(0, BLOCKS - 1) as j:
                section_loads(j, LOOP)
            section_loads(BLOCKS - 1, LAST)

        @block.gpsimd
        def _(pool):
            def load_ids(j):
                pool.dma_start(ids_sb[:], ids[bass.ds(j * ROWS, ROWS), :]).then_inc(ids_loaded, 16)

            def gather(f):
                pool.indirect_dma_start(
                    out=emb[:, f * DIM:(f + 1) * DIM], out_offset=None, in_=tables[f],
                    in_offset=bass.IndirectOffsetOnAxis(ap=ids_sb[:, f:f + 1].bitcast(u32), axis=0),
                ).then_inc(gathered, 16)

            def low_part(section, u, before):
                pool.wait_ge(hi_ready, before.splits + u.s + 1)
                slot = section.p_slot(u)
                nc.gpsimd.tensor_tensor(prod_lo[:, slot, :], prod[:, slot, :],
                                        prod_hi[:, section.hi_slot(u), :].bitcast(f32),
                                        ALU.subtract).then_inc(pool_lo_ready, 1)

            def section_lows(j, section, coming=None, start=0):
                before = Counts(section, j)
                lows = [u for u in section.units if u.low_by_pool]
                late = [u.n for u in lows if coming is not None and u.n >= start]
                done = 0
                for u in lows:
                    if late and u is lows[0]:
                        pool.wait_ge(gathered, 16 * FIELDS * coming)
                        pool.sem_inc(pool_waited, 1)
                        load_ids(coming)
                    low_part(section, u, before)
                    if late and u.n == late[0]:
                        pool.wait_ge(turned_ready, TURNS * coming)
                        pool.sem_inc(pool_waited, 1)
                        pool.wait_ge(ids_loaded, 16 * (coming + 1))
                        pool.sem_inc(pool_waited, 1)
                    if u.n in late:
                        after = min([n for n in late if n > u.n], default=len(section.units))
                        upto = FIELDS * (after - late[0]) // (len(section.units) - late[0])
                        for f in range(done, upto):
                            gather(f)
                        done = upto

            load_ids(0)
            pool.wait_ge(ids_loaded, 16)
            for f in range(FIELDS):
                gather(f)
            section_lows(None, FIRST, 1)
            with pool.Fori(0, BLOCKS - 2) as j:
                section_lows(j, LOOP, j + 2, LOOP.begins(1)[0] + TURN_AT + TURNS + GATHER_LAG)
            section_lows(BLOCKS - 2, LOOP)
            section_lows(BLOCKS - 1, LAST)

        @block.vector
        def _(dve):
            dve.wait_ge(cin_weights_loaded, 16 * N_CIN)
            for t in range(UNITS_0):
                if (0, t) in whole_list:
                    to = w_whole[:, whole_list.index((0, t)), :]
                else:
                    to = raw[:, split_list.index((0, t)), :]
                nc.vector.tensor_tensor(to, raw_direct[:, t, :], raw_mirror[:, t, :],
                                        ALU.add).then_inc(pair_sums_ready, 1)
            dve.wait_ge(pair_sums_ready, UNITS_0)
            for k in range(len(split_list)):
                nc.vector.tensor_copy(w_hi[:, k, :], raw[:, k, :]).then_inc(w_hi_ready, 1)
            dve.wait_ge(w_hi_ready, len(split_list))
            for k, (l, t) in enumerate(split_list):
                at = SHORT_AT if (l, t) == (0, SHORT_0) else slice(0, rows_of(l, t))
                to = w_hi if (l, t) == (0, SHORT_0) else w_lo
                last = nc.vector.tensor_tensor(to[at, k, :], raw[at, k, :], w_hi[at, k, :].bitcast(f32),
                                               ALU.subtract)
            last.then_inc(weights_ready, 1)

            def low_part(section, u, before):
                dve.wait_ge(prod_ready, before.groups + u.g + 1)
                dve.wait_ge(hi_ready, before.splits + u.s + 1)
                ring = section.hi_slot(u)
                at, lo = slice(0, u.rows), prod_lo[:, section.p_slot(u), :]
                if u.rows == 64:
                    lo = prod_hi[64:128, ring, :]
                elif u.rows == 32:
                    at, lo = SHORT_AT, prod_hi[32:64, ring, :]
                nc.vector.tensor_tensor(lo, prod[at, section.p_slot(u), :], prod_hi[at, ring, :].bitcast(f32),
                                        ALU.subtract).then_inc(vector_lo_ready, 1)

            def reduce_half(j, n, which, half, phase_no):
                src = (direct01, direct2)[which]
                dst = (sums, part_sums)[half]
                dve.wait_ge(phase_taken, phase_no)
                nc.vector.tensor_reduce(dst[:, which, :], src[:].rearrange("p (d b) -> p b d", b=ROWS),
                                        AX.X, ALU.add).then_inc(half_reduced, 1)
                if half == B:
                    dve.wait_ge(half_reduced, j * 4 + n)
                    nc.vector.tensor_tensor(sums[:, which, :], sums[:, which, :],
                                            part_sums[:, which, :], ALU.add).then_inc(sums_ready, 1)

            def section_products(j, section, events):
                before = Counts(section, j)
                waiting = []
                for group in section.groups:
                    u, n = group[0], len(group)
                    first_slot = section.p_slot(u)
                    to = prod[:, first_slot:first_slot + n, :]
                    no = halves_before(section, u.phase, j)
                    if u.i == 0 and section.needs_last_phase(u.phase):
                        while waiting:
                            low_part(section, waiting.pop(0), before)
                    if u.i == 0 and u.layer > 0:
                        half = section.phases[u.phase][1]
                        source = next((p for p in reversed(range(u.phase))
                                       if section.phases[p] == (u.layer - 1, half)), -1)
                        kept = sum(section.phases[p][0] < 2 for p in range(source + 1))
                        dve.wait_ge(x_taken, before.kept + kept)
                    if u.layer == 0:
                        if u.i == 0:
                            dve.wait_ge(pair_rep_loaded, (no + 1) * 16)
                        for item in (LAST_0, OWN_LAST) if u.t == LAST_0 else [x.t for x in group]:
                            slot = PAIR_SLOT[item]
                            loads = list(PAIR_SLOT.values()).count(slot)
                            dve.wait_ge(shift_loaded[slot], (no * loads + (item in RELOADED) + 1) * 16)
                        slot = PAIR_SLOT.get(u.t, 0)
                        shifted = pair_shift[:, slot:slot + n, :]
                        own = pair_rep[:].unsqueeze(1).to_broadcast([128, n, HALF])
                        if u.t == SHORT_0:
                            dve.wait_ge(pair_short_loaded, (no + 1) * 16)
                            to, own, shifted = to[SHORT_AT, 0, :], pair_short, shifted[SHORT_AT, 0, :]
                        elif u.t == LAST_0:
                            own = pair_shift[:, PAIR_SLOT[OWN_LAST]:PAIR_SLOT[OWN_LAST] + 1, :]
                        operands = own, shifted
                    else:
                        if u.layer == 1:
                            g = next(g for g, load in enumerate(LOADS) if u.t in load)
                            dve.wait_ge(x0_rep_loaded[g], (no + 1) * (16 * (u.rows // KEPT)))
                        at = slice(0, u.rows)
                        to = to[at]
                        x = (x1, x2)[u.layer - 1][at, :].unsqueeze(1).to_broadcast([u.rows, n, HALF])
                        operands = x, x0_rep[at, u.t:u.t + n, :]
                    olds = [section.before(x, section.p_slot, lambda x: True) for x in group]
                    old = [x.n for x in olds if x is not None]
                    if old:
                        dve.wait_ge(unit_done, before.units + max(old) + 1)
                    nc.vector.tensor_tensor(to, *operands, ALU.mult).then_inc(prod_ready, 1)
                    while waiting and waiting[0].g <= u.g - LAG:
                        low_part(section, waiting.pop(0), before)
                    waiting += [x for x in group if x.split and not x.low_by_pool]
                    for x in group:
                        for args in events.get((x.phase, x.i), ()):
                            reduce_half(*args)
                for u in waiting:
                    low_part(section, u, before)

            section_products(None, FIRST, {})

            def loop_events(j, section):
                phases = Counts(section, j).phases
                ev = {(0, 6): [(j, 1, 0, A, phases)],
                      (2, 6): [(j, 2, 1, A, phases + 2)],
                      (3, 6): [(j, 3, 0, B, phases + 3)]}
                if section is LOOP:
                    ev[(5, 6)] = [(j, 4, 1, B, phases + 5)]
                return ev

            with dve.Fori(0, BLOCKS - 1) as j:
                section_products(j, LOOP, loop_events(j, LOOP))
            j = BLOCKS - 1
            section_products(j, LAST, loop_events(j, LAST))
            reduce_half(j, 4, 1, B, Counts(LAST, j).phases + 4)

        @block.scalar
        def _(act):
            def take_turned(j, g):
                n = j * TURNS + g
                act.wait_ge(turned_ready, n + 1)
                nc.scalar.copy(x0_sb[:, g * BANK:(g + 1) * BANK],
                               turned[0:2 * FIELDS, g, :]).then_inc(turned_taken, 1)

            def last_phase(section, ph):
                layer = section.phases[ph][0] if ph >= 0 else 1
                return layer, acc[:, ph % 2, :], bias_sb[:, layer:layer + 1]

            def take_kept(section, ph, units):
                layer, z, b = last_phase(section, ph)
                act.wait_ge(unit_done, units + section.ends(ph))
                if layer < 2:
                    x, kept = ((x1, slice(0, KEPT)), (x2, slice(KEPT, 128)))[layer]
                    nc.scalar.activation(x[0:KEPT, :], z[kept, :], ACT.Relu, bias=b[kept, :])
                    nc.scalar.activation(x[KEPT:128, :], z[kept, :], ACT.Relu,
                                         bias=b[kept, :]).then_inc(x_taken, 1)

            def take_results(section, ph, j):
                layer, z, b = last_phase(section, ph)
                if layer == 0 and section is not FIRST:
                    n = 1 if section.phases[ph][1] == B else 3
                    act.wait_ge(half_reduced, j * 4 + n)
                if layer == 2 and section is LOOP:
                    act.wait_ge(x0_stored, 32 * (j + 2))
                at = (slice(KEPT, 128), slice(0, KEPT), slice(0, 128))[layer]
                to = direct2 if layer == 2 else direct01
                nc.scalar.activation(to[at, :], z[at, :], ACT.Relu, bias=b[at, :]).then_inc(phase_taken, 1)

            def top_relu1(j):
                act.wait_ge(top1_done, j + 1)
                for m in range(TOP1 // 128):
                    last = nc.scalar.activation(h1[:, m, :], top_a[:, m, :], ACT.Relu, bias=tb1_sb[:, m:m + 1])
                last.then_inc(h1_ready, 1)

            def top_relu2(j):
                act.wait_ge(top2_done, j + 1)
                for m in range(TOP2 // 128):
                    last = nc.scalar.activation(h2[:, m, :], top_b[:, m, :], ACT.Relu, bias=tb2_sb[:, m:m + 1])
                last.then_inc(h2_ready, 1)

            def store_y(j):
                act.wait_ge(top3_done, j + 1)
                nc.scalar.copy(y_sb[:], top_b[:, TOP2 // 128, 0:1]).then_inc(y_ready, 1)
                act.wait_ge(y_ready, j + 1)
                act.dma_start(out_rows[bass.ds(j, 1), :, :].rearrange("a b c -> (a b) c"), y_sb[:]).then_inc(y_stored, 16)

            def section_scalar(j, section, events):
                before = Counts(section, j)
                units = before.units
                for u in section.units:
                    if u.i == 0 and section.needs_last_phase(u.phase):
                        take_kept(section, u.phase - 1, units)
                        take_results(section, u.phase - 1, j)
                    if u.split:
                        if (old := section.before(u, section.hi_slot, lambda x: x.split)) is not None:
                            act.wait_ge(unit_done, units + old.n + 1)
                        act.wait_ge(prod_ready, before.groups + u.g + 1)
                        hi, p = prod_hi[:, section.hi_slot(u), :], prod[:, section.p_slot(u), :]
                        at = SHORT_AT if u.rows == 32 else slice(0, u.rows)
                        nc.scalar.copy(hi[at, :], p[at, :]).then_inc(hi_ready, 1)
                        if u.rows == 32:
                            nc.scalar.copy(hi[0:32, :], p[at, :]).then_inc(stack_ready, 1)
                    if not section.needs_last_phase(u.phase) and not (section is FIRST and u.phase == 0):
                        if u.i == KEPT_AT:
                            take_kept(section, u.phase - 1, units)
                        if u.i == RESULTS_AT:
                            take_results(section, u.phase - 1, j)
                    for step in events.get((u.phase, u.i), ()):
                        step()

            act.wait_ge(consts_loaded, 16 * N_CONSTS)
            for g in range(TURNS):
                take_turned(0, g)
            section_scalar(None, FIRST, {})
            with act.Fori(0, BLOCKS - 1) as j:
                ev = {(1, TURN_AT + 5 + g): [lambda g=g: take_turned(j + 1, g)] for g in range(TURNS)}
                ev[(5, 10)] = [lambda: top_relu1(j)]
                ev[(5, 14)] = [lambda: top_relu2(j)]
                ev[(5, 17)] = [lambda: store_y(j)]
                section_scalar(j, LOOP, ev)
                act.wait_ge(y_stored, 16 * (j + 1))
            j = BLOCKS - 1
            section_scalar(j, LAST, {})
            take_kept(LAST, 3, Counts(LAST, j).units)
            take_results(LAST, 3, j)
            top_relu1(j)
            top_relu2(j)
            store_y(j)
            act.wait_ge(y_stored, 16 * BLOCKS)

        @block.tensor
        def _(pe):
            emb_by_dim = emb[:].rearrange("p (r q) -> p q r", q=DIM // 2)

            def turn(j, g, phase_no=None):
                if g == 0:
                    pe.wait_ge(gathered, (j + 1) * (16 * FIELDS))
                    if phase_no is not None:
                        pe.wait_ge(phase_taken, phase_no)
                for q in range(4):
                    last = nc.tensor.transpose(turned[0:2 * FIELDS, g, q * ROWS:(q + 1) * ROWS],
                                               emb_by_dim[:, 4 * g + q, :], eye_sb[:])
                last.then_inc(turned_ready, 1)

            def top_layer1(j):
                pe.wait_ge(sums_ready, 2 * (j + 1))
                pe.wait_ge(context_loaded, 16 * (j + 1))
                for m in range(TOP1 // 128):
                    cols = slice(m * 128, (m + 1) * 128)
                    nc.tensor.matmul(top_a[:, m, :], top1_sb[:, 0, cols], sums[:, 0, :], start=True, stop=False)
                    nc.tensor.matmul(top_a[:, m, :], top1_sb[:, 1, cols], sums[:, 1, :], start=False, stop=False)
                    last = nc.tensor.matmul(top_a[:, m, :], top1c_sb[:, cols], context_sb[:],
                                            start=False, stop=True)
                last.then_inc(top1_done, 1)

            def top_layer2(j):
                pe.wait_ge(h1_ready, j + 1)
                for m in range(TOP2 // 128):
                    for k in range(TOP1 // 128):
                        last = nc.tensor.matmul(top_b[:, m, :], top2_sb[:, k, m * 128:(m + 1) * 128],
                                                h1[:, k, :], start=k == 0, stop=k == TOP1 // 128 - 1)
                last.then_inc(top2_done, 1)

            def top_layer3(j):
                pe.wait_ge(h2_ready, j + 1)
                for k in range(TOP2 // 128):
                    last = nc.tensor.matmul(top_b[:, TOP2 // 128, 0:1], h2[:, k, :], top3_sb[:, k:k + 1],
                                            start=k == 0, stop=k == TOP2 // 128 - 1)
                last.then_inc(top3_done, 1)

            def section_matmuls(j, section, events):
                before = Counts(section, j)
                for u in section.units:
                    first, last_unit = u.i == 0, u.i == UNITS[u.layer] - 1
                    if first and section is not FIRST:
                        pe.wait_ge(phase_taken, before.phases + (u.phase - 1))
                        if u.phase == 2 and section is LOOP:
                            pe.wait_ge(turned_taken, TURNS * (j + 2))
                    slot = u.phase % 2
                    if u.split:
                        k = split_list.index((u.layer, u.t))
                        hi = section.hi_slot(u)
                        pe.wait_ge(hi_ready, before.splits + u.s + 1)
                        steps = {128: [(w_hi, prod_hi, hi, 128), (w_lo, prod_hi, hi, 128),
                                       (w_hi, prod_lo, section.p_slot(u), 128)],
                                 64: [(w_lo, prod_hi, hi, 64), (w_hi, prod_hi, hi, 128)],
                                 32: [(w_hi, prod_hi, hi, 96)]}[u.rows]
                        if u.rows == 32:
                            pe.wait_ge(stack_ready, halves_before(section, u.phase, j) + 1)
                    else:
                        k = whole_list.index((u.layer, u.t))
                        pe.wait_ge(prod_ready, before.groups + u.g + 1)
                        steps = [(w_whole, prod, section.p_slot(u), 128)]
                    for i, (w, p, ring, rows) in enumerate(steps):
                        if u.split and i == len(steps) - 1:
                            if u.low_by_pool:
                                pe.wait_ge(pool_lo_ready, before.pool_lows + u.pool_lows + 1)
                            else:
                                pe.wait_ge(vector_lo_ready, before.vector_lows + (u.s - u.pool_lows) + 1)
                        for c in range(HALF // BANK):
                            cols = slice(c * BANK, (c + 1) * BANK)
                            last = nc.tensor.matmul(acc[:, slot, cols], w[0:rows, k, :], p[0:rows, ring, cols],
                                                    start=first and i == 0,
                                                    stop=last_unit and i == len(steps) - 1)
                    last.then_inc(unit_done, 1)
                    for step in events.get((u.phase, u.i), ()):
                        step()

            pe.wait_ge(consts_loaded, 16 * N_CONSTS)
            for g in range(TURNS):
                turn(0, g)
            pe.wait_ge(turned_taken, TURNS)
            pe.wait_ge(weights_ready, 1)
            section_matmuls(None, FIRST, {})
            with pe.Fori(0, BLOCKS - 1) as j:
                phases = Counts(LOOP, j).phases
                ev = {(1, TURN_AT + g): [lambda g=g: turn(j + 1, g, phases + 1)] for g in range(TURNS)}
                ev[(5, 5)] = [lambda: top_layer1(j)]
                ev[(5, 9)] = [lambda: top_layer2(j)]
                ev[(5, 13)] = [lambda: top_layer3(j)]
                section_matmuls(j, LOOP, ev)
                pe.wait_ge(y_ready, j + 1)
            j = BLOCKS - 1
            section_matmuls(j, LAST, {})
            top_layer1(j)
            top_layer2(j)
            top_layer3(j)


def pair_indices():
    none = FIELDS * FIELDS
    one = np.full((128, UNITS_0), none)
    other = one.copy()

    def put(row, t, i, shift):
        k = (i + shift) % FIELDS
        if i < FIELDS:
            one[row, t] = FIELDS * i + k
            if shift > 0:
                other[row, t] = FIELDS * k + i

    for t, first in FIRST_SHIFT.items():
        for row in range(128):
            put(row, t, row // 4, first + row % 4)
    for row in range(128):
        put(row, LAST_0, 32 + row % 8, row // 8)
    for row in range(96):
        put(row, SHORT_0, 32 + row % 32 // 4, 16 + row % 4)
    return one, other


def unit_weights(w, t):
    rows = w[first_field(t) * KEPT:first_field(t) * KEPT + rows_of(1, t)]
    return np.concatenate([rows, rows]) if t == SHORT_K else rows


def kernel(**inputs):
    import concourse.bacc as bacc
    from concourse.bass_utils import run_bass_kernel_spmd

    a = {name: np.asarray(value) for name, value in inputs.items()}
    one, other = pair_indices()
    flat0 = np.concatenate([a["L0_rec_w0"].reshape(FIELDS * FIELDS, SIZE), np.zeros((1, SIZE), np.float32)])
    w1 = a["L0_rec_w1"].reshape(FIELDS * KEPT, SIZE)
    w12 = {1: np.concatenate([w1[:, KEPT:], w1[:, :KEPT]], axis=1),
           2: a["L0_rec_w2"].reshape(FIELDS * KEPT, SIZE)}
    b1 = a["L0_rec_b1"]
    top1 = a["W_top1"]
    arrays = {
        "ids": a["ids"],
        **{f"tbl_{f}": a[f"tbl_{f}"] for f in range(FIELDS)},
        "w0": flat0[one],
        "w0_mirror": flat0[other],
        "w12_whole": np.stack([unit_weights(w12[l], t) for l in (1, 2) for t in range(UNITS_K)
                               if t not in SPLIT[l]], axis=1),
        "w12_split": np.stack([unit_weights(w12[l], t) for l in (1, 2) for t in range(UNITS_K)
                               if t in SPLIT[l]], axis=1),
        "bias0": a["L0_rec_b0"].reshape(SIZE, 1),
        "bias1": np.concatenate([b1[KEPT:], b1[:KEPT]]).reshape(SIZE, 1),
        "bias2": a["L0_rec_b2"].reshape(SIZE, 1),
        "top1": np.stack([np.concatenate([top1[KEPT:2 * KEPT], top1[:KEPT]]),
                          top1[2 * KEPT:4 * KEPT]], axis=1),
        "top1_context": top1[4 * KEPT:],
        "top2": a["W_top2"].reshape(TOP1 // 128, 128, TOP2).transpose(1, 0, 2),
        "top3": a["W_top3"].reshape(TOP2 // 128, 128).T,
        "top_bias1": a["b_top1"].reshape(TOP1 // 128, 128).T,
        "top_bias2": a["b_top2"].reshape(TOP2 // 128, 128).T,
        "context": a["dense_ctx"].reshape(BLOCKS, ROWS, CONTEXT).transpose(0, 2, 1),
        "eye": np.eye(128, dtype=np.float32),
    }
    arrays = {name: np.ascontiguousarray(x) for name, x in arrays.items()}
    nc = bacc.Bacc("TRN2", target_bir_lowering=False, num_devices=1)
    aps = {name: nc.dram_tensor(name, x.shape, mybir.dt.from_np(x.dtype), kind="ExternalInput").ap()
           for name, x in arrays.items()}
    out = nc.dram_tensor("y", (BATCH, 1), mybir.dt.float32, kind="ExternalOutput").ap()
    tables = [aps.pop(f"tbl_{f}") for f in range(FIELDS)]
    build(nc, aps.pop("ids"), tables, **aps, out=out)
    result = run_bass_kernel_spmd(nc, [arrays], core_ids=[0])
    return result.results[0]["y"]
```
